# Optimizing a Trainium2 kernel written in Bass

```python
import numpy as np
import jax
import jax.numpy as jnp

def _softmax(x, axis=-1):
    return jax.nn.softmax(x, axis=axis)

def _gelu(x):
    return jax.nn.gelu(x, approximate=True)

def _silu(x):
    return jax.nn.silu(x)

def _sigmoid(x):
    return jax.nn.sigmoid(x)

def _layernorm(x, axis=-1, eps=1e-05):
    m = jnp.mean(x, axis=axis, keepdims=True)
    v = jnp.var(x, axis=axis, keepdims=True)
    return (x - m) / jnp.sqrt(v + eps)

def _scatter_add(tgt, idx, src, axis=0):
    return tgt.at[idx].add(src)

def _segment_sum(src, seg, n):
    return jax.ops.segment_sum(src, seg, n)
kernel_name = 'mk_dlrm_tower_d1_rec_r8_2b71e3'

def setup_inputs(seed: int=0):
    np.random.seed(seed)
    _w = jnp.asarray

    def _rec_inputs():
        import jax
        import jax.numpy as jnp
        _tk = jax.random.key(seed)
        ids = jnp.stack([jax.random.randint(jax.random.fold_in(_tk, 200 + f), (2048,), 0, v, jnp.int32) for f, v in enumerate([1000, 1000, 125000, 1250, 1000, 12500, 12500, 12500, 1000, 1000, 1000, 12500, 1000, 1250, 12500, 12500, 1000, 1250, 12500, 1000, 12500, 1000, 12500, 1250, 1000, 1000])], axis=1)
        tbl_0 = 0.05 * jax.random.normal(jax.random.fold_in(_tk, 500 + 0), (1000, 128), jnp.float32)
        tbl_1 = 0.05 * jax.random.normal(jax.random.fold_in(_tk, 500 + 1), (1000, 128), jnp.float32)
        tbl_2 = 0.05 * jax.random.normal(jax.random.fold_in(_tk, 500 + 2), (125000, 128), jnp.float32)
        tbl_3 = 0.05 * jax.random.normal(jax.random.fold_in(_tk, 500 + 3), (1250, 128), jnp.float32)
        tbl_4 = 0.05 * jax.random.normal(jax.random.fold_in(_tk, 500 + 4), (1000, 128), jnp.float32)
        tbl_5 = 0.05 * jax.random.normal(jax.random.fold_in(_tk, 500 + 5), (12500, 128), jnp.float32)
        tbl_6 = 0.05 * jax.random.normal(jax.random.fold_in(_tk, 500 + 6), (12500, 128), jnp.float32)
        tbl_7 = 0.05 * jax.random.normal(jax.random.fold_in(_tk, 500 + 7), (12500, 128), jnp.float32)
        tbl_8 = 0.05 * jax.random.normal(jax.random.fold_in(_tk, 500 + 8), (1000, 128), jnp.float32)
        tbl_9 = 0.05 * jax.random.normal(jax.random.fold_in(_tk, 500 + 9), (1000, 128), jnp.float32)
        tbl_10 = 0.05 * jax.random.normal(jax.random.fold_in(_tk, 500 + 10), (1000, 128), jnp.float32)
        tbl_11 = 0.05 * jax.random.normal(jax.random.fold_in(_tk, 500 + 11), (12500, 128), jnp.float32)
        tbl_12 = 0.05 * jax.random.normal(jax.random.fold_in(_tk, 500 + 12), (1000, 128), jnp.float32)
        tbl_13 = 0.05 * jax.random.normal(jax.random.fold_in(_tk, 500 + 13), (1250, 128), jnp.float32)
        tbl_14 = 0.05 * jax.random.normal(jax.random.fold_in(_tk, 500 + 14), (12500, 128), jnp.float32)
        tbl_15 = 0.05 * jax.random.normal(jax.random.fold_in(_tk, 500 + 15), (12500, 128), jnp.float32)
        tbl_16 = 0.05 * jax.random.normal(jax.random.fold_in(_tk, 500 + 16), (1000, 128), jnp.float32)
        tbl_17 = 0.05 * jax.random.normal(jax.random.fold_in(_tk, 500 + 17), (1250, 128), jnp.float32)
        tbl_18 = 0.05 * jax.random.normal(jax.random.fold_in(_tk, 500 + 18), (12500, 128), jnp.float32)
        tbl_19 = 0.05 * jax.random.normal(jax.random.fold_in(_tk, 500 + 19), (1000, 128), jnp.float32)
        tbl_20 = 0.05 * jax.random.normal(jax.random.fold_in(_tk, 500 + 20), (12500, 128), jnp.float32)
        tbl_21 = 0.05 * jax.random.normal(jax.random.fold_in(_tk, 500 + 21), (1000, 128), jnp.float32)
        tbl_22 = 0.05 * jax.random.normal(jax.random.fold_in(_tk, 500 + 22), (12500, 128), jnp.float32)
        tbl_23 = 0.05 * jax.random.normal(jax.random.fold_in(_tk, 500 + 23), (1250, 128), jnp.float32)
        tbl_24 = 0.05 * jax.random.normal(jax.random.fold_in(_tk, 500 + 24), (1000, 128), jnp.float32)
        tbl_25 = 0.05 * jax.random.normal(jax.random.fold_in(_tk, 500 + 25), (1000, 128), jnp.float32)
        _rk = jax.random.fold_in(_tk, 7)
        r_dense_features = -0.000520686 + 1.00062 * jax.random.normal(jax.random.fold_in(_rk, 101), (2048, 128), jnp.float32)
        W_top1 = 0.0405887 * jax.random.normal(jax.random.fold_in(_tk, 801), (607, 512), jnp.float32)
        W_top2 = 0.0441942 * jax.random.normal(jax.random.fold_in(_tk, 802), (512, 256), jnp.float32)
        W_top3 = 0.0625 * jax.random.normal(jax.random.fold_in(_tk, 803), (256, 1), jnp.float32)
        b_top1 = jnp.zeros((512,), jnp.float32)
        b_top2 = jnp.zeros((256,), jnp.float32)
        return (r_dense_features, ids, tbl_0, tbl_1, tbl_2, tbl_3, tbl_4, tbl_5, tbl_6, tbl_7, tbl_8, tbl_9, tbl_10, tbl_11, tbl_12, tbl_13, tbl_14, tbl_15, tbl_16, tbl_17, tbl_18, tbl_19, tbl_20, tbl_21, tbl_22, tbl_23, tbl_24, tbl_25, W_top1, b_top1, W_top2, b_top2, W_top3)
    r_dense_features, ids, tbl_0, tbl_1, tbl_2, tbl_3, tbl_4, tbl_5, tbl_6, tbl_7, tbl_8, tbl_9, tbl_10, tbl_11, tbl_12, tbl_13, tbl_14, tbl_15, tbl_16, tbl_17, tbl_18, tbl_19, tbl_20, tbl_21, tbl_22, tbl_23, tbl_24, tbl_25, W_top1, b_top1, W_top2, b_top2, W_top3 = _rec_inputs()

    def _L0_rec_setup():
        import jax, jax.numpy as jnp
        import numpy as np
        B, F, D = (2048, 26, 128)
        key = jax.random.key(seed)
        k1, k2 = jax.random.split(key)
        dense_features = jax.random.normal(k1, (B, D), dtype=jnp.float32)
        sparse_values = jax.random.normal(k2, (B, F, D), dtype=jnp.float32)
        return {'dense_features': dense_features, 'sparse_values': sparse_values}
    _L0_rec_all = _L0_rec_setup()
    _L0_rec_in = {k: v for k, v in _L0_rec_all.items() if k in ()}
    del _L0_rec_all
    return {'r_dense_features': r_dense_features, 'ids': ids, 'tbl_0': tbl_0, 'tbl_1': tbl_1, 'tbl_2': tbl_2, 'tbl_3': tbl_3, 'tbl_4': tbl_4, 'tbl_5': tbl_5, 'tbl_6': tbl_6, 'tbl_7': tbl_7, 'tbl_8': tbl_8, 'tbl_9': tbl_9, 'tbl_10': tbl_10, 'tbl_11': tbl_11, 'tbl_12': tbl_12, 'tbl_13': tbl_13, 'tbl_14': tbl_14, 'tbl_15': tbl_15, 'tbl_16': tbl_16, 'tbl_17': tbl_17, 'tbl_18': tbl_18, 'tbl_19': tbl_19, 'tbl_20': tbl_20, 'tbl_21': tbl_21, 'tbl_22': tbl_22, 'tbl_23': tbl_23, 'tbl_24': tbl_24, 'tbl_25': tbl_25, 'W_top1': W_top1, 'b_top1': b_top1, 'W_top2': W_top2, 'b_top2': b_top2, 'W_top3': W_top3}

def reference(r_dense_features, ids, tbl_0, tbl_1, tbl_2, tbl_3, tbl_4, tbl_5, tbl_6, tbl_7, tbl_8, tbl_9, tbl_10, tbl_11, tbl_12, tbl_13, tbl_14, tbl_15, tbl_16, tbl_17, tbl_18, tbl_19, tbl_20, tbl_21, tbl_22, tbl_23, tbl_24, tbl_25, W_top1, b_top1, W_top2, b_top2, W_top3):
    import jax
    import jax.numpy as jnp

    def _L0_rec_ref(dense_features, sparse_values):
        import jax, jax.numpy as jnp
        import numpy as np
        B, F, D = (2048, 26, 128)
        sd = jnp.einsum('bfd,bd->bf', sparse_values, dense_features)
        ss = jnp.einsum('bfd,bgd->bfg', sparse_values, sparse_values)
        iu, ju = jnp.triu_indices(F, k=1)
        pairs = ss[:, iu, ju]
        return jnp.concatenate([dense_features, sd, pairs], axis=1)
    e = jnp.stack([tbl_0[ids[:, 0]], tbl_1[ids[:, 1]], tbl_2[ids[:, 2]], tbl_3[ids[:, 3]], tbl_4[ids[:, 4]], tbl_5[ids[:, 5]], tbl_6[ids[:, 6]], tbl_7[ids[:, 7]], tbl_8[ids[:, 8]], tbl_9[ids[:, 9]], tbl_10[ids[:, 10]], tbl_11[ids[:, 11]], tbl_12[ids[:, 12]], tbl_13[ids[:, 13]], tbl_14[ids[:, 14]], tbl_15[ids[:, 15]], tbl_16[ids[:, 16]], tbl_17[ids[:, 17]], tbl_18[ids[:, 18]], tbl_19[ids[:, 19]], tbl_20[ids[:, 20]], tbl_21[ids[:, 21]], tbl_22[ids[:, 22]], tbl_23[ids[:, 23]], tbl_24[ids[:, 24]], tbl_25[ids[:, 25]]], axis=1)
    z = _L0_rec_ref(r_dense_features, e)
    z = z.reshape(z.shape[0], -1)
    h = jnp.concatenate([z, r_dense_features], axis=1)
    h = jnp.maximum(h @ W_top1 + b_top1, 0.0)
    h = jnp.maximum(h @ W_top2 + b_top2, 0.0)
    y = h @ W_top3
    return y

_drawn_inputs = setup_inputs


def setup_inputs(seed=0):
    import zlib

    import numpy as np

    out = dict(_drawn_inputs(seed))
    spreads = {'b_top1': (0.0, 0.1), 'b_top2': (0.0, 0.1)}
    factors = {}
    for name, (base, spread) in spreads.items():
        noise = np.random.default_rng([zlib.crc32(name.encode()), seed]).standard_normal(out[name].shape)
        drawn = base * np.exp(spread * noise) if base else spread * noise
        out[name] = jnp.asarray(drawn.astype(out[name].dtype))
    for name, factor in factors.items():
        out[name] = (out[name] * factor).astype(out[name].dtype)
    return out
```

```python
import concourse.bass as bass
from concourse import mybir
from concourse.alu_op_type import AluOpType as ALU
from contextlib import ExitStack

B, F, D = 2048, 26, 128
ROWS = [1000, 1000, 125000, 1250, 1000, 12500, 12500, 12500, 1000, 1000, 1000, 12500, 1000,
        1250, 12500, 12500, 1000, 1250, 12500, 1000, 12500, 1000, 12500, 1250, 1000, 1000]
N1, N2 = 512, 256
P = 128

NF = F + 1
SMALL = min(ROWS)
ONEHOT = [f for f in range(F) if ROWS[f] == SMALL][:9]
GATHERED = [f for f in range(F) if f not in ONEHOT]
NO, NG = len(ONEHOT), len(GATHERED)

CH = 256
TILES = CH // P
NCH = B // CH
Q = 4
QS = CH // Q
UNIT_FEATURES = [0] + [f + 1 for f in GATHERED]
UNITS = len(UNIT_FEATURES) // 2
assert UNITS == NO and 2 * UNITS == len(UNIT_FEATURES)
RING = 6
RPP = 8
TP = SMALL // RPP
FS = 32
GPU = 8
GUNITS = QS // GPU
NJ = NF - 1
PAIRS = NF * (NF - 1) // 2
ZC = -(-PAIRS // P)
IG = 3
IGROUPS = NO // IG
DMA = 16


def pair_runs():
    row, runs = 0, []
    for i in range(NF - 1):
        j = i
        while j < NJ:
            block, p0 = divmod(row, P)
            m = min(NJ - j, P - p0)
            runs.append((i, j, m, block, p0))
            row += m
            j += m
    return runs


RUNS = pair_runs()
Z_DMAS = len(RUNS) + 1


def dlrm_tower(nc, dense, dense_t, idx, ids_t, tables, w1, b1, w2, b2, w3, y):
    fp32, fp32r, i32 = mybir.dt.float32, mybir.dt.float32r, mybir.dt.int32
    ACT = mybir.ActivationFunctionType
    zd = nc.dram_tensor("dots_scratch", (2, 32, NJ, CH), fp32, kind="Internal").ap()

    ctx = ExitStack()
    with ctx:
        def sb(name, shape, dt):
            return ctx.enter_context(nc.sbuf_tensor(name, shape, dt))

        def ps(name, shape, dt):
            return ctx.enter_context(nc.psum_tensor(name, shape, dt))

        def sem(name):
            return ctx.enter_context(nc.semaphore(name))

        feat = sb("feat", [P, 2, QS, Q, FS], fp32)
        table_hi = sb("table_hi", [P, NO, RPP * D], fp32r)
        table_lo = sb("table_lo", [P, NO, RPP * D], fp32r)
        onehot = sb("onehot", [P, 2, RPP, CH], fp32r)
        ids_bc = sb("ids_bc", [P, NO, CH], i32)
        rows = sb("rows", [P, RING, 2, TILES, D], fp32)
        idx_sb = sb("idx_sb", [P, 2, NG * TILES], i32)
        dots = sb("dots", [P, 2, NJ * QS], fp32)
        zt = sb("zt", [P, ZC + 1, CH], fp32)
        w1_sb = sb("w1_sb", [P, ZC + 1, N1], fp32)
        w2_sb = sb("w2_sb", [P, N1 // P, N2], fp32)
        w3_sb = sb("w3_sb", [P, N2 // P], fp32)
        b1_sb = sb("b1_sb", [P, N1 // P], fp32)
        b2_sb = sb("b2_sb", [P, N2 // P], fp32)
        h1 = sb("h1", [P, N1 // P, CH], fp32)
        h2 = sb("h2", [P, N2 // P, CH], fp32)
        y_sb = sb("y_sb", [1, 2, CH], fp32)
        row_i = sb("row_i", [P, RPP], i32)
        row_f = sb("row_f", [P, RPP], fp32)
        ident = sb("ident", [P, P], fp32)
        diag = h1[:, 2, 0:P].bitcast(i32)
        w1_dense2 = h1[:, 0:2, :].rearrange("p a b -> p (a b)")

        feat1 = feat[:, 1].rearrange("p g q f -> p (g q f)")
        dots_flat = dots[:].rearrange("p a x -> p (a x)")
        IN_FEAT = (Q * QS * FS) // (RPP * D)

        def raw_table(u):
            if u < IN_FEAT:
                return feat1[:, u * RPP * D:(u + 1) * RPP * D]
            return dots_flat[:, (u - IN_FEAT) * RPP * D:(u - IN_FEAT + 1) * RPP * D]

        tr_ps = ps("tr_ps", [P, 2, CH], fp32)
        oh_ps = ps("oh_ps", [P, 512], fp32)
        dot_ps = ps("dot_ps", [P, 2, 2, 512], fp32)
        mlp_ps = ps("mlp_ps", [P, 2, 512], fp32)

        idx_loaded = [sem(f"idx_loaded{p}") for p in range(2)]
        ids_loaded = [sem(f"ids_loaded{j}") for j in range(IGROUPS)]
        rows_loaded = [sem(f"rows_loaded{r}") for r in range(RING)]
        dense_loaded = [sem(f"dense_loaded{p}") for p in range(2)]
        table_loaded = [sem(f"table_loaded{u}") for u in range(NO)]
        weights_loaded = sem("weights_loaded")
        slot_free = sem("slot_free")
        pads_zeroed = sem("pads_zeroed")
        iotas_made = sem("iotas_made")
        row_f_made = sem("row_f_made")
        ident_made = sem("ident_made")
        hi_made = sem("hi_made")
        lo_made = sem("lo_made")
        w1_summed = sem("w1_summed")
        onehot_made = sem("onehot_made")
        transposed = sem("transposed")
        transposed_out = sem("transposed_out")
        looked_up = sem("looked_up")
        looked_up_out = sem("looked_up_out")
        dots_done = sem("dots_done")
        dots_out_act = sem("dots_out_act")
        dots_out_dve = sem("dots_out_dve")
        dots_stored = sem("dots_stored")
        z_loaded = sem("z_loaded")
        l1_done = sem("l1_done")
        h1_made = sem("h1_made")
        l2_done = sem("l2_done")
        h2_made = sem("h2_made")
        l3_done = sem("l3_done")
        y_made = sem("y_made")
        y_stored = [sem(f"y_stored{p}") for p in range(2)]

        def chunk(h, par):
            return 2 * h + par

        def feat_view(par, f0, nf, step):
            v = feat[:, par].rearrange("p g q f -> p f q g")
            return v[:, f0:f0 + step * (nf - 1) + 1:step]

        def dot_copy(par, v, q):
            p = slice(32 * q, 32 * (q + 1))
            dst = dots[p, par, :].rearrange("p (j g) -> p g j", j=NJ)[:, v * GPU:(v + 1) * GPU, :]
            src = dot_ps[p, v % 2, :, 0:GPU // 2 * Q * NJ].rearrange("p k (g q j) -> p k g q j", q=Q, j=NJ)
            return dst.rearrange("p (k g) j -> p k g j", k=2), src[:, :, :, q, :]

        block = ctx.enter_context(nc.Block())

        @block.sync
        def _(sp):
            def load_idx(h, par):
                n = chunk(h, par)
                sp.dma_start(idx_sb[:, par, :],
                             idx[bass.ds(n, 1)].rearrange("a p x -> (a p) x")).then_inc(idx_loaded[par], DMA)

            def load_ids(h, par, j):
                n = chunk(h, par)
                src = ids_t[bass.ds(n, 1), j * IG:(j + 1) * IG, :].rearrange("a f b -> a (f b)")
                sp.dma_start(ids_bc[:, j * IG:(j + 1) * IG, :].rearrange("p f b -> p (f b)"),
                             src.broadcast_to([P, IG * CH])).then_inc(ids_loaded[j], DMA)

            def load_dense(h, par):
                n = chunk(h, par)
                slot = (UNITS * par) % RING
                sp.dma_start(rows[:, slot, 0],
                             dense[bass.ds(n, 1)].rearrange("a t p d -> p (a t) d")
                             ).then_inc(dense_loaded[par], DMA)

            def load_table(u):
                raw = raw_table(u)
                src = tables[ONEHOT[u]].rearrange("(r c) d -> r (c d)", c=RPP)
                sp.dma_start(raw[0:120], src[0:120]).then_inc(table_loaded[u], DMA)
                sp.dma_start(raw[120:TP], src[120:TP]).then_inc(table_loaded[u], DMA)

            def next_chunk_loads(h, par, ids=True, indices=True):
                n = chunk(h, par)
                hn, parn = (h, 1) if par == 0 else (h + 1, 0)
                if ids:
                    for j in range(IGROUPS):
                        sp.wait_ge(onehot_made, n * NO + (j + 1) * IG)
                        load_ids(hn, parn, j)
                        if j == 1:
                            sp.wait_ge(transposed, (n + 1) * UNITS - RING + 1)
                            load_dense(hn, parn)
                if indices:
                    sp.wait_ge(transposed, (n + 1) * UNITS)
                    load_idx(h + 1, par)

            def make_z(h, par):
                n = chunk(h, par)
                sp.wait_ge(dots_out_act, GUNITS * (n + 1))
                sp.wait_ge(dots_out_dve, GUNITS * (n + 1))
                for q in range(Q):
                    sp.dma_start(zd[par, :, :, q * QS:(q + 1) * QS],
                                 dots[32 * q:32 * (q + 1), par, :].rearrange("p (j g) -> p j g", j=NJ)
                                 ).then_inc(dots_stored, DMA)
                if not (isinstance(n, int) and n == 0):
                    sp.wait_ge(l1_done, N1 // P * n)
                sp.dma_start(zt[:, ZC, :], dense_t[bass.ds(n, 1)].rearrange("a p b -> (a p) b")
                             ).then_inc(z_loaded, DMA)
                sp.wait_ge(dots_stored, Q * DMA * (n + 1))
                for i, j, m, block, p0 in RUNS:
                    sp.dma_start(zt[p0:p0 + m, block, :], zd[par, i, j:j + m, :]).then_inc(z_loaded, DMA)

            def store_y(h, par):
                n = chunk(h, par)
                sp.wait_ge(y_made, n + 1)
                sp.dma_start(y[bass.ds(n, 1), :], y_sb[:, par, :]).then_inc(y_stored[par], DMA)

            load_idx(0, 0)
            sp.wait_ge(pads_zeroed, 1)
            load_table(0)
            load_ids(0, 0, 0)
            load_dense(0, 0)
            load_table(1)
            load_table(2)
            load_idx(0, 1)
            load_ids(0, 0, 1)
            load_ids(0, 0, 2)
            next_chunk_loads(0, 0)
            next_chunk_loads(0, 1)
            make_z(0, 0)
            with sp.Fori(1, NCH // 2 - 1) as h:
                next_chunk_loads(h, 0)
                make_z(h - 1, 1)
                store_y(h - 1, 0)
                next_chunk_loads(h, 1)
                make_z(h, 0)
                store_y(h - 1, 1)
            last = NCH // 2 - 1
            next_chunk_loads(last, 0, indices=False)
            make_z(last - 1, 1)
            store_y(last - 1, 0)
            make_z(last, 0)
            store_y(last - 1, 1)
            make_z(last, 1)
            store_y(last, 0)
            store_y(last, 1)
            for par in range(2):
                sp.wait_ge(y_stored[par], DMA * (NCH // 2))

        @block.gpsimd
        def _(pool):
            nc.gpsimd.iota(row_i[:], [[1, RPP]], base=0, channel_multiplier=RPP)
            nc.gpsimd.iota(diag, [[1, P]], base=0, channel_multiplier=-1).then_inc(iotas_made, 1)

            def gathers(h, par):
                pool.wait_ge(idx_loaded[par], DMA * (h + 1))
                pool.sem_inc(slot_free, 1)
                for u in range(UNITS):
                    slot = (UNITS * par + u) % RING
                    if not (isinstance(h, int) and h == 0 and UNITS * par + u < RING):
                        pool.wait_ge(transposed, chunk(h, par) * UNITS + u - RING + 1)
                        pool.sem_inc(slot_free, 1)
                    for k in range(2):
                        g = 2 * u + k - 1
                        if g < 0:
                            continue
                        for t in range(TILES):
                            nc.gpsimd.indirect_dma_start(
                                rows[:, slot, k, t, :], None, tables[GATHERED[g]],
                                bass.IndirectOffsetOnAxis(
                                    ap=idx_sb[:, par, g * TILES + t:g * TILES + t + 1], axis=0),
                            ).then_inc(rows_loaded[slot], DMA)

            gathers(0, 0)
            gathers(0, 1)
            with pool.Fori(1, NCH // 2) as h:
                gathers(h, 0)
                gathers(h, 1)

        @block.scalar
        def _(act):
            act.wait_ge(pads_zeroed, 1)
            for u in range(3, NO):
                raw = raw_table(u)
                src = tables[ONEHOT[u]].rearrange("(r c) d -> r (c d)", c=RPP)
                act.dma_start(raw[0:120], src[0:120]).then_inc(table_loaded[u], DMA)
                act.dma_start(raw[120:TP], src[120:TP]).then_inc(table_loaded[u], DMA)
            z0 = D
            for c in range(ZC):
                m = min(P, PAIRS - c * P)
                act.dma_start(w1_sb[0:m, c, :], w1[z0 + c * P:z0 + c * P + m, :]).then_inc(weights_loaded, DMA)
            act.dma_start(w1_sb[:, ZC, :], w1[0:D, :]).then_inc(weights_loaded, DMA)
            act.wait_ge(ident_made, 1)
            act.dma_start(w1_dense2, w1[D + PAIRS:, :]).then_inc(weights_loaded, DMA)
            act.dma_start(w2_sb[:], w2.rearrange("(c p) n -> p c n", p=P)).then_inc(weights_loaded, DMA)
            act.dma_start(w3_sb[:], w3).then_inc(weights_loaded, DMA)
            act.dma_start(b1_sb[:], b1).then_inc(weights_loaded, DMA)
            act.dma_start(b2_sb[:], b2).then_inc(weights_loaded, DMA)

            def split_hi(u):
                act.wait_ge(table_loaded[u], 2 * DMA)
                nc.scalar.activation(table_hi[0:TP, u, :], raw_table(u)[0:TP], ACT.Copy).then_inc(hi_made, 1)

            def transposed_to_feat(h, par, u):
                act.wait_ge(transposed, chunk(h, par) * UNITS + u + 1)
                fa, fb = UNIT_FEATURES[2 * u:2 * u + 2]
                nc.scalar.activation(feat_view(par, fa, 2, fb - fa),
                                     tr_ps[:].rearrange("p f (q g) -> p f q g", q=Q),
                                     ACT.Copy).then_inc(transposed_out, 1)

            def looked_up_to_feat(h, par, u):
                act.wait_ge(looked_up, chunk(h, par) * NO + u + 1)
                nc.scalar.activation(feat_view(par, ONEHOT[u] + 1, 1, 1)[:, 0],
                                     oh_ps[:, 0:CH].rearrange("p (q g) -> p q g", q=Q),
                                     ACT.Copy).then_inc(looked_up_out, 1)

            def dots_to_sbuf(h, par, v):
                act.wait_ge(dots_done, chunk(h, par) * GUNITS + v + 1)
                for q in range(Q // 2):
                    last = nc.scalar.activation(*dot_copy(par, v, q), ACT.Copy)
                last.then_inc(dots_out_act, 1)

            def relu1(h, par, x):
                act.wait_ge(l1_done, chunk(h, par) * (N1 // P) + x + 1)
                nc.scalar.activation(h1[:, x, :], mlp_ps[:, x % 2, 0:CH], ACT.Relu,
                                     bias=b1_sb[:, x:x + 1]).then_inc(h1_made, 1)

            def relu2(h, par, x):
                act.wait_ge(l2_done, chunk(h, par) * (N2 // P) + x + 1)
                nc.scalar.activation(h2[:, x, :], mlp_ps[:, x, 0:CH], ACT.Relu,
                                     bias=b2_sb[:, x:x + 1]).then_inc(h2_made, 1)

            def output(h, par):
                n = chunk(h, par)
                act.wait_ge(l3_done, n + 1)
                if not (isinstance(h, int) and h == 0):
                    act.wait_ge(y_stored[par], DMA * h)
                nc.scalar.activation(y_sb[:, par, :], mlp_ps[0:1, 0, 0:CH],
                                     ACT.Copy).then_inc(y_made, 1)

            def slot(h, par, lookups=True, dot=None, mlp=None):
                for u in range(UNITS):
                    if lookups:
                        if isinstance(h, int) and h == 0 and par == 0:
                            split_hi(u)
                        transposed_to_feat(h, par, u)
                    if mlp and u == UNITS - 1:
                        relu2(*mlp, 0)
                        relu2(*mlp, 1)
                    if lookups:
                        looked_up_to_feat(h, par, u)
                    if mlp and u == UNITS - 1:
                        output(*mlp)
                    if dot and u < GUNITS:
                        dots_to_sbuf(*dot, u)
                    if mlp and 4 <= u < 4 + N1 // P:
                        relu1(*mlp, u - 4)

            slot(0, 0)
            act.wait_ge(weights_loaded, 9 * DMA)
            act.wait_ge(w1_summed, 1)
            slot(0, 1, dot=(0, 0))
            with act.Fori(1, NCH // 2) as h:
                slot(h, 0, dot=(h - 1, 1), mlp=(h - 1, 0))
                slot(h, 1, dot=(h, 0), mlp=(h - 1, 1))
            last = NCH // 2 - 1
            for v in range(GUNITS):
                dots_to_sbuf(last, 1, v)
            for par in range(2):
                slot(last, par, lookups=False, mlp=(last, par))

        @block.vector
        def _(dve):
            nc.vector.memset(feat[:, :, :, :, NF:FS], 0.0).then_inc(pads_zeroed, 1)
            dve.wait_ge(iotas_made, 1)
            nc.vector.tensor_copy(row_f[:], row_i[:]).then_inc(row_f_made, 1)
            nc.vector.tensor_scalar(ident[:], diag, 0.0, None, ALU.is_equal).then_inc(ident_made, 1)
            dve.wait_ge(row_f_made, 1)

            def split_lo(u):
                dve.wait_ge(hi_made, u + 1)
                nc.vector.tensor_tensor(table_lo[0:TP, u, :], raw_table(u)[0:TP],
                                        table_hi[0:TP, u, :].bitcast(fp32), ALU.subtract).then_inc(lo_made, 1)

            def make_onehot(h, par, u):
                n = chunk(h, par)
                if u % IG == 0:
                    dve.wait_ge(ids_loaded[u // IG], DMA * (n + 1))
                first = isinstance(h, int) and h == 0 and par == 0
                if not (first and u < 2):
                    dve.wait_ge(looked_up, n * NO + u - 1)
                buf = (NO * par + u) % 2
                for c in range(RPP):
                    last = nc.vector.tensor_scalar(onehot[0:TP, buf, c, :], ids_bc[0:TP, u, :],
                                                   row_f[0:TP, c:c + 1], None, ALU.is_equal)
                last.then_inc(onehot_made, 1)

            def dots_to_sbuf(h, par, v):
                dve.wait_ge(dots_done, chunk(h, par) * GUNITS + v + 1)
                for q in range(Q // 2, Q):
                    last = nc.vector.tensor_copy(*dot_copy(par, v, q))
                last.then_inc(dots_out_dve, 1)

            def slot(h, par, dot=None):
                for u in range(NO):
                    if isinstance(h, int) and h == 0 and par == 0:
                        split_lo(u)
                    make_onehot(h, par, u)
                    if dot and u >= 1:
                        dots_to_sbuf(*dot, u - 1)

            slot(0, 0)
            dve.wait_ge(weights_loaded, 9 * DMA)
            nc.vector.tensor_tensor(w1_sb[:, ZC, :], w1_sb[:, ZC, :], w1_dense2, ALU.add).then_inc(w1_summed, 1)
            slot(0, 1, dot=(0, 0))
            with dve.Fori(1, NCH // 2) as h:
                slot(h, 0, dot=(h - 1, 1))
                slot(h, 1, dot=(h, 0))
            for v in range(GUNITS):
                dots_to_sbuf(NCH // 2 - 1, 1, v)

        @block.tensor
        def _(pe):
            def is_first(h, par, u=0):
                return isinstance(h, int) and h == 0 and par == 0 and u == 0

            def transposes(h, par, u):
                at = UNITS * par + u
                slot = at % RING
                loads = [TILES * (1 if a % UNITS == 0 else 2) for a in range(slot, 2 * UNITS, RING)]
                pe.wait_ge(rows_loaded[slot], DMA * sum(loads) * h + DMA * sum(loads[:at // RING + 1]))
                if u == 0:
                    pe.wait_ge(dense_loaded[par], DMA * (h + 1))
                if not is_first(h, par, u):
                    pe.wait_ge(transposed_out, chunk(h, par) * UNITS + u)
                for k in range(2):
                    for t in range(TILES):
                        last = nc.tensor.transpose(tr_ps[:, k, t * P:(t + 1) * P], rows[:, slot, k, t, :], ident[:])
                last.then_inc(transposed, 1)

            def lookup(h, par, u):
                n = chunk(h, par)
                if isinstance(h, int) and h == 0 and par == 0:
                    pe.wait_ge(lo_made, u + 1)
                pe.wait_ge(onehot_made, n * NO + u + 1)
                if not is_first(h, par, u):
                    pe.wait_ge(looked_up_out, n * NO + u)
                buf = (NO * par + u) % 2
                for part in (table_lo, table_hi):
                    for c in range(RPP):
                        last = nc.tensor.matmul(oh_ps[:, 0:CH], part[0:TP, u, c * D:(c + 1) * D],
                                                onehot[0:TP, buf, c, :],
                                                start=(part is table_lo and c == 0),
                                                stop=(part is table_hi and c == RPP - 1))
                last.then_inc(looked_up, 1)

            def dot_products(h, par, v):
                n = chunk(h, par)
                if v == 0:
                    pe.wait_ge(transposed_out, UNITS * (n + 1))
                    pe.wait_ge(looked_up_out, NO * (n + 1))
                if not (isinstance(n, int) and n == 0 and v < 2):
                    pe.wait_ge(dots_out_act, n * GUNITS + v - 1)
                    pe.wait_ge(dots_out_dve, n * GUNITS + v - 1)
                for k in range(2):
                    for gi in range(GPU // 2):
                        g = v * GPU + k * (GPU // 2) + gi
                        last = nc.tensor.matmul(dot_ps[:, v % 2, k, gi * Q * NJ:(gi + 1) * Q * NJ],
                                                feat[:, par, g].rearrange("p q f -> p (q f)"),
                                                feat[:, par, g, :, 1:NF],
                                                start=True, stop=True)
                last.then_inc(dots_done, 1)

            def layer1(h, par, x):
                n = chunk(h, par)
                first = isinstance(n, int) and n == 0
                if x == 0:
                    pe.wait_ge(z_loaded, DMA * Z_DMAS * (n + 1))
                    if not first:
                        pe.wait_ge(y_made, n)
                if x == 1 and not first:
                    pe.wait_ge(h2_made, n * (N2 // P))
                if x >= 2:
                    pe.wait_ge(h1_made, n * (N1 // P) + x - 1)
                for c in range(ZC + 1):
                    m = PAIRS - c * P if c == ZC - 1 else P
                    last = nc.tensor.matmul(mlp_ps[:, x % 2, 0:CH], w1_sb[0:m, c, x * P:(x + 1) * P],
                                            zt[0:m, c, :], start=(c == 0), stop=(c == ZC))
                last.then_inc(l1_done, 1)

            def layer2(h, par):
                n = chunk(h, par)
                pe.wait_ge(h1_made, (N1 // P) * (n + 1))
                for x in range(N2 // P):
                    for c in range(N1 // P):
                        last = nc.tensor.matmul(mlp_ps[:, x, 0:CH], w2_sb[:, c, x * P:(x + 1) * P],
                                                h1[:, c, :], start=(c == 0), stop=(c == N1 // P - 1))
                    last.then_inc(l2_done, 1)

            def layer3(h, par):
                n = chunk(h, par)
                pe.wait_ge(h2_made, (N2 // P) * (n + 1))
                for c in range(N2 // P):
                    last = nc.tensor.matmul(mlp_ps[0:1, 0, 0:CH], w3_sb[:, c:c + 1], h2[:, c, :],
                                            start=(c == 0), stop=(c == N2 // P - 1))
                last.then_inc(l3_done, 1)

            def slot(h, par, dot=None, mlp=None):
                for u in range(UNITS):
                    transposes(h, par, u)
                    if mlp and u == UNITS - 1:
                        layer2(*mlp)
                    lookup(h, par, u)
                    if mlp and u == UNITS - 1:
                        layer3(*mlp)
                    if dot and u < GUNITS:
                        dot_products(*dot, u)
                    if mlp and 4 <= u < 4 + N1 // P:
                        layer1(*mlp, u - 4)

            pe.wait_ge(ident_made, 1)
            slot(0, 0)
            pe.wait_ge(weights_loaded, 9 * DMA)
            pe.wait_ge(w1_summed, 1)
            slot(0, 1, dot=(0, 0))
            with pe.Fori(1, NCH // 2) as h:
                slot(h, 0, dot=(h - 1, 1), mlp=(h - 1, 0))
                slot(h, 1, dot=(h, 0), mlp=(h - 1, 1))
            last = NCH // 2 - 1
            for v in range(GUNITS):
                dot_products(last, 1, v)
            for par in range(2):
                for x in range(N1 // P):
                    layer1(last, par, x)
                layer2(last, par)
                layer3(last, par)


def kernel(**inputs):
    import numpy as np
    import concourse.bacc as bacc
    from concourse.bass_utils import run_bass_kernel_spmd

    nc = bacc.Bacc("TRN2", target_bir_lowering=False, num_devices=1, dynamic_dma_scratch_size=8192)
    ids = np.ascontiguousarray(inputs["ids"])
    dense = np.ascontiguousarray(inputs["r_dense_features"])
    arrays = {
        "dense": dense.reshape(NCH, TILES, P, D),
        "dense_t": dense.reshape(NCH, CH, D).transpose(0, 2, 1),
        "idx": ids[:, GATHERED].reshape(NCH, TILES, P, NG).transpose(0, 2, 3, 1).reshape(NCH, P, NG * TILES),
        "ids_t": ids[:, ONEHOT].reshape(NCH, CH, NO).transpose(0, 2, 1),
    }
    for f in range(F):
        arrays[f"tbl_{f}"] = inputs[f"tbl_{f}"]
    arrays["W_top1"], arrays["W_top2"] = inputs["W_top1"], inputs["W_top2"]
    for name in ("b_top1", "b_top2", "W_top3"):
        arrays[name] = np.asarray(inputs[name]).reshape(-1, P).T
    arrays = {name: np.ascontiguousarray(a) for name, a in arrays.items()}
    aps = {name: nc.dram_tensor(name + "_dram", a.shape, mybir.dt.from_np(a.dtype), kind="ExternalInput").ap()
           for name, a in arrays.items()}
    y = nc.dram_tensor("y_dram", (NCH, CH), mybir.dt.float32, kind="ExternalOutput").ap()
    dlrm_tower(nc, aps["dense"], aps["dense_t"], aps["idx"], aps["ids_t"], [aps[f"tbl_{f}"] for f in range(F)],
               aps["W_top1"], aps["b_top1"], aps["W_top2"], aps["b_top2"], aps["W_top3"], y)
    r = run_bass_kernel_spmd(nc, [{name + "_dram": a for name, a in arrays.items()}], core_ids=[0])
    return r.results[0]["y_dram"].reshape(B, 1)
```

```python
import concourse.bass as bass
from concourse import mybir
from concourse.alu_op_type import AluOpType as ALU
from contextlib import ExitStack

B, F, D = 2048, 26, 128
ROWS = [1000, 1000, 125000, 1250, 1000, 12500, 12500, 12500, 1000, 1000, 1000, 12500, 1000,
        1250, 12500, 12500, 1000, 1250, 12500, 1000, 12500, 1000, 12500, 1250, 1000, 1000]
N1, N2 = 512, 256
P = 128

NF = F + 1
SMALL = min(ROWS)
ONEHOT = [f for f in range(F) if ROWS[f] == SMALL][:7]
GATHERED = [f for f in range(F) if f not in ONEHOT]
NO, NG = len(ONEHOT), len(GATHERED)

CH = 256
TILES = CH // P
NCH = B // CH
Q = 4
NI = NF - 1
QS = CH // Q
UNITS = -(-NG // 2)
UNIT = [GATHERED[2 * u:2 * u + 2] for u in range(UNITS)]
RPP = 8
TP = SMALL // RPP
FS = 32
GPU = 8
GUNITS = QS // GPU
NJ = NF - 1
PAIRS = NF * (NF - 1) // 2
ZC = -(-PAIRS // P)
IDS = [(0, 4), (4, NO)]
ROWS_IN_DOTS = {1: 0, 4: 1, 7: 2}
ROWS_IN_LOOKUPS = {u: u + 3 for u in range(NO)}
LAYER2_AT, LAYER3_AT = 4, 6
WEIGHT_DMAS = ZC + 6
DMA = 16


def pair_runs():
    row, runs = 0, []
    for i in range(NF - 1):
        j = i
        while j < NJ:
            block, p0 = divmod(row, P)
            m = min(NJ - j, P - p0)
            runs.append((i, j, m, block, p0))
            row += m
            j += m
    return runs


RUNS = pair_runs()
Z_DMAS = len(RUNS) + 1


def dlrm_tower(nc, dense_t, idx, pair_idx, ids_t, tables, w1, b1, w2, b2, w3, y):
    fp32, fp32r, i32 = mybir.dt.float32, mybir.dt.float32r, mybir.dt.int32
    ACT = mybir.ActivationFunctionType
    dots_dram = nc.dram_tensor("dots_scratch", (2, NI, NJ, CH), fp32, kind="Internal").ap()
    dots_last = nc.dram_tensor("dots_last_scratch", (NI * NJ, CH), fp32, kind="Internal").ap()

    ctx = ExitStack()
    with ctx:
        def sb(name, shape, dt):
            return ctx.enter_context(nc.sbuf_tensor(name, shape, dt))

        def ps(name, shape, dt):
            return ctx.enter_context(nc.psum_tensor(name, shape, dt))

        def sem(name):
            return ctx.enter_context(nc.semaphore(name))

        feat = sb("feat", [P, 2, QS, Q, FS], fp32)
        table_hi = sb("table_hi", [P, NO, RPP * D], fp32r)
        table_lo = sb("table_lo", [P, NO, RPP * D], fp32r)
        onehot = sb("onehot", [P, 2, RPP, CH], fp32r)
        ids_bc = sb("ids_bc", [P, NO, CH], i32)
        rows = sb("rows", [P, UNITS, 2, TILES, D], fp32)
        dense_sb = sb("dense_sb", [P, 2, CH], fp32)
        pair_idx_sb = sb("pair_idx_sb", [P, ZC], i32)
        idx_sb = sb("idx_sb", [P, 2, NG * TILES], i32)
        dots = sb("dots", [P, 2, NJ * QS], fp32)
        zt = sb("zt", [P, ZC + 1, CH], fp32)
        w1_sb = sb("w1_sb", [P, ZC + 1, N1], fp32)
        w2_sb = sb("w2_sb", [P, N1 // P, N2], fp32)
        w3_sb = sb("w3_sb", [P, N2 // P], fp32)
        b1_sb = sb("b1_sb", [P, N1 // P], fp32)
        b2_sb = sb("b2_sb", [P, N2 // P], fp32)
        h1 = sb("h1", [P, N1 // P, CH], fp32)
        h2 = sb("h2", [P, N2 // P, CH], fp32)
        y_sb = sb("y_sb", [P, B // P], fp32)
        row_i = sb("row_i", [P, 1], i32)
        row_f = sb("row_f", [P, 1], fp32)
        ident = sb("ident", [P, P], fp32)
        ids_local = ids_bc[:].bitcast(fp32)
        diag = h1[:, 2, 0:P].bitcast(i32)
        w1_dense2 = h1[:, 0:2, :].rearrange("p a b -> p (a b)")

        feat1 = feat[:, 1].rearrange("p g q f -> p (g q f)")

        def raw_table(u):
            if u == 0:
                return dots[:, 0, 0:RPP * D]
            return feat1[:, (u - 1) * RPP * D:u * RPP * D]

        tr_ps = ps("tr_ps", [P, 2, CH], fp32)
        oh_ps = ps("oh_ps", [P, 512], fp32)
        dot_ps = ps("dot_ps", [P, 2, 2, 512], fp32)
        mlp_ps = ps("mlp_ps", [P, 2, 512], fp32)

        idx_loaded = [sem(f"idx_loaded{p}") for p in range(2)]
        ids_loaded = [sem(f"ids_loaded{j}") for j in range(len(IDS))]
        rows_loaded = [sem(f"rows_loaded{u}") for u in range(UNITS)]
        dense_loaded = [sem(f"dense_loaded{p}") for p in range(2)]
        table_loaded = [sem(f"table_loaded{u}") for u in range(NO)]
        pair_idx_loaded = sem("pair_idx_loaded")
        pairs_gathered = sem("pairs_gathered")
        last_stored = sem("last_stored")
        dense_out = sem("dense_out")
        weights_loaded = sem("weights_loaded")
        slot_free = sem("slot_free")
        pads_zeroed = sem("pads_zeroed")
        pads0_zeroed = sem("pads0_zeroed")
        iotas_made = sem("iotas_made")
        ids_shifted = sem("ids_shifted")
        row_f_made = sem("row_f_made")
        ident_made = sem("ident_made")
        hi_made = sem("hi_made")
        lo_made = sem("lo_made")
        w1_summed = sem("w1_summed")
        onehot_made = sem("onehot_made")
        transposed = sem("transposed")
        transposed_out = sem("transposed_out")
        looked_up = sem("looked_up")
        looked_up_out = sem("looked_up_out")
        dots_done = sem("dots_done")
        dots_out_act = sem("dots_out_act")
        dots_out_dve = sem("dots_out_dve")
        dots_stored = sem("dots_stored")
        z_loaded = sem("z_loaded")
        l1_done = sem("l1_done")
        h1_made = sem("h1_made")
        l2_done = sem("l2_done")
        h2_made = sem("h2_made")
        l3_done = sem("l3_done")
        y_made = sem("y_made")
        y_stored = sem("y_stored")

        def chunk(h, par):
            return 2 * h + par

        def feat_view(par, f0, nf, step):
            v = feat[:, par].rearrange("p g q f -> p f q g")
            return v[:, f0:f0 + step * (nf - 1) + 1:step]

        def dot_copy(par, v, q):
            p = slice(32 * q, 32 * q + NI)
            dst = dots[p, par, :].rearrange("p (j g) -> p g j", j=NJ)[:, v * GPU:(v + 1) * GPU, :]
            src = dot_ps[p, v % 2, :, 0:GPU // 2 * Q * NJ].rearrange("p k (g q j) -> p k g q j", q=Q, j=NJ)
            return dst.rearrange("p (k g) j -> p k g j", k=2), src[:, :, :, q, :]

        block = ctx.enter_context(nc.Block())

        @block.sync
        def _(sp):
            def load_idx(h, par):
                sp.dma_start(idx_sb[:, par, :], idx[bass.ds(chunk(h, par), 1)].rearrange("a p x -> (a p) x")
                             ).then_inc(idx_loaded[par], DMA)

            def load_ids(h, par, j):
                a, b = IDS[j]
                src = ids_t[bass.ds(chunk(h, par), 1), a:b, :].rearrange("a f b -> a (f b)")
                sp.dma_start(ids_bc[:, a:b, :].rearrange("p f b -> p (f b)"),
                             src.broadcast_to([P, (b - a) * CH])).then_inc(ids_loaded[j], DMA)

            def load_dense(h, par):
                sp.dma_start(dense_sb[:, par, :], dense_t[bass.ds(chunk(h, par), 1)].rearrange("a p b -> (a p) b")
                             ).then_inc(dense_loaded[par], DMA)

            def load_table(u):
                raw = raw_table(u)
                src = tables[ONEHOT[u]].rearrange("(r c) d -> r (c d)", c=RPP)
                sp.dma_start(raw[0:120], src[0:120]).then_inc(table_loaded[u], DMA)
                sp.dma_start(raw[120:TP], src[120:TP]).then_inc(table_loaded[u], DMA)

            def next_dense(h, par):
                n = chunk(h, par)
                if not (isinstance(n, int) and n == 0):
                    sp.wait_ge(dense_out, n)
                load_dense(*((h, 1) if par == 0 else (h + 1, 0)))

            def next_ids(h, par):
                for j in range(len(IDS)):
                    sp.wait_ge(onehot_made, (chunk(h, par) + 1) * NO + IDS[j][1])
                    load_ids(h + 1, par, j)

            def next_idx(h, par):
                sp.wait_ge(transposed, (chunk(h, par) + 1) * UNITS)
                load_idx(h + 1, par)

            def make_z(h, par, last=False):
                n = chunk(h, par)
                sp.wait_ge(dots_out_act, GUNITS * (n + 1))
                sp.wait_ge(dots_out_dve, GUNITS * (n + 1))
                dst = dots_last.rearrange("(i j) b -> i j b", j=NJ) if last else dots_dram[par]
                stored = last_stored if last else dots_stored
                for q in range(Q):
                    sp.dma_start(dst[:, :, q * QS:(q + 1) * QS],
                                 dots[32 * q:32 * q + NI, par, :].rearrange("p (j g) -> p j g", j=NJ)
                                 ).then_inc(stored, DMA)
                if not (isinstance(n, int) and n == 0):
                    sp.wait_ge(l1_done, N1 // P * n)
                sp.dma_start(zt[:, ZC, :], dense_t[bass.ds(n, 1)].rearrange("a p b -> (a p) b")
                             ).then_inc(z_loaded, DMA)
                if last:
                    return
                sp.wait_ge(dots_stored, Q * DMA * (n + 1))
                for i, j, m, block, p0 in RUNS:
                    sp.dma_start(zt[p0:p0 + m, block, :], dots_dram[par, i, j:j + m, :]).then_inc(z_loaded, DMA)

            load_idx(0, 0)
            load_table(0)
            load_ids(0, 0, 0)
            sp.wait_ge(pads_zeroed, 1)
            for u in range(1, 4):
                load_table(u)
            load_ids(0, 0, 1)
            for u in range(4, NO):
                load_table(u)
            load_dense(0, 0)
            load_idx(0, 1)
            for j in range(len(IDS)):
                sp.wait_ge(onehot_made, IDS[j][1])
                load_ids(0, 1, j)
            for c in range(ZC):
                m = min(P, PAIRS - c * P)
                sp.dma_start(w1_sb[0:m, c, :], w1[D + c * P:D + c * P + m, :]).then_inc(weights_loaded, DMA)
            sp.dma_start(w1_sb[:, ZC, :], w1[0:D, :]).then_inc(weights_loaded, DMA)
            sp.wait_ge(ident_made, 1)
            sp.dma_start(w1_dense2, w1[D + PAIRS:, :]).then_inc(weights_loaded, DMA)
            sp.dma_start(w2_sb[:], w2.rearrange("(c p) n -> p c n", p=P)).then_inc(weights_loaded, DMA)
            sp.dma_start(w3_sb[:], w3).then_inc(weights_loaded, DMA)
            sp.dma_start(b1_sb[:], b1).then_inc(weights_loaded, DMA)
            sp.dma_start(b2_sb[:], b2).then_inc(weights_loaded, DMA)
            sp.dma_start(pair_idx_sb[:], pair_idx).then_inc(pair_idx_loaded, DMA)
            next_dense(0, 0)
            next_ids(0, 0)
            next_idx(0, 0)
            next_dense(0, 1)
            make_z(0, 0)
            next_ids(0, 1)
            next_idx(0, 1)
            with sp.Fori(1, NCH // 2 - 1) as h:
                next_dense(h, 0)
                make_z(h - 1, 1)
                next_ids(h, 0)
                next_idx(h, 0)
                next_dense(h, 1)
                make_z(h, 0)
                next_ids(h, 1)
                next_idx(h, 1)
            last = NCH // 2 - 1
            next_dense(last, 0)
            make_z(last - 1, 1)
            make_z(last, 0)
            make_z(last, 1, last=True)
            sp.wait_ge(y_made, NCH)
            sp.dma_start(y, y_sb[:]).then_inc(y_stored, DMA)
            sp.wait_ge(y_stored, DMA)

        @block.gpsimd
        def _(pool):
            nc.gpsimd.iota(row_i[:], [[1, 1]], base=0, channel_multiplier=RPP)
            nc.gpsimd.iota(diag, [[1, P]], base=0, channel_multiplier=-1).then_inc(iotas_made, 1)

            def gathers(h, par):
                pool.wait_ge(idx_loaded[par], DMA * (h + 1))
                pool.sem_inc(slot_free, 1)
                for u in range(UNITS):
                    if not (isinstance(h, int) and h == 0 and par == 0):
                        pool.wait_ge(transposed, (chunk(h, par) - 1) * UNITS + u + 1)
                        pool.sem_inc(slot_free, 1)
                    for k in range(len(UNIT[u])):
                        g = 2 * u + k
                        for t in range(TILES):
                            nc.gpsimd.indirect_dma_start(
                                rows[:, u, k, t, :], None, tables[GATHERED[g]],
                                bass.IndirectOffsetOnAxis(
                                    ap=idx_sb[:, par, g * TILES + t:g * TILES + t + 1], axis=0),
                            ).then_inc(rows_loaded[u], DMA)

            gathers(0, 0)
            gathers(0, 1)
            with pool.Fori(1, NCH // 2) as h:
                gathers(h, 0)
                gathers(h, 1)
            pool.wait_ge(pair_idx_loaded, DMA)
            pool.wait_ge(l1_done, N1 // P * (NCH - 1))
            pool.wait_ge(last_stored, Q * DMA)
            for c in range(ZC):
                m = min(P, PAIRS - c * P)
                nc.gpsimd.indirect_dma_start(
                    zt[0:m, c, :], None, dots_last,
                    bass.IndirectOffsetOnAxis(ap=pair_idx_sb[0:m, c:c + 1], axis=0)).then_inc(pairs_gathered, DMA)

        @block.scalar
        def _(act):
            def split_hi(u):
                act.wait_ge(table_loaded[u], 2 * DMA)
                nc.scalar.activation(table_hi[0:TP, u, :], raw_table(u)[0:TP], ACT.Copy).then_inc(hi_made, 1)

            def dense_to_feat(h, par):
                act.wait_ge(dense_loaded[par], DMA * (h + 1))
                nc.scalar.activation(feat_view(par, 0, 1, 1)[:, 0],
                                     dense_sb[:, par, :].rearrange("p (q g) -> p q g", q=Q),
                                     ACT.Copy).then_inc(dense_out, 1)

            def transposed_to_feat(h, par, u):
                act.wait_ge(transposed, chunk(h, par) * UNITS + u + 1)
                m, step = len(UNIT[u]), UNIT[u][-1] - UNIT[u][0]
                nc.scalar.activation(feat_view(par, UNIT[u][0] + 1, m, max(step, 1)),
                                     tr_ps[:, 0:m].rearrange("p f (q g) -> p f q g", q=Q),
                                     ACT.Copy).then_inc(transposed_out, 1)

            def looked_up_to_feat(h, par, u):
                act.wait_ge(looked_up, chunk(h, par) * NO + u + 1)
                nc.scalar.activation(feat_view(par, ONEHOT[u] + 1, 1, 1)[:, 0],
                                     oh_ps[:, 0:CH].rearrange("p (q g) -> p q g", q=Q),
                                     ACT.Copy).then_inc(looked_up_out, 1)

            def dots_to_sbuf(h, par, v):
                act.wait_ge(dots_done, chunk(h, par) * GUNITS + v + 1)
                for q in range(Q // 2):
                    last = nc.scalar.activation(*dot_copy(par, v, q), ACT.Copy)
                last.then_inc(dots_out_act, 1)

            def relu1(h, par, x):
                act.wait_ge(l1_done, chunk(h, par) * (N1 // P) + x + 1)
                nc.scalar.activation(h1[:, x, :], mlp_ps[:, x % 2, 0:CH], ACT.Relu,
                                     bias=b1_sb[:, x:x + 1]).then_inc(h1_made, 1)

            def relu2(h, par, x):
                act.wait_ge(l2_done, chunk(h, par) * (N2 // P) + x + 1)
                nc.scalar.activation(h2[:, x, :], mlp_ps[:, x, 0:CH], ACT.Relu,
                                     bias=b2_sb[:, x:x + 1]).then_inc(h2_made, 1)

            def output(h, par):
                n = chunk(h, par)
                act.wait_ge(l3_done, n + 1)
                nc.scalar.activation(y_sb[:, bass.ds(n * TILES, TILES)], mlp_ps[:, 0, 0:TILES],
                                     ACT.Copy).then_inc(y_made, 1)

            def mlp_step(h, par, u):
                if u < N1 // P:
                    relu1(h, par, u)
                if u == LAYER2_AT:
                    for x in range(N2 // P):
                        relu2(h, par, x)
                if u == LAYER3_AT:
                    output(h, par)

            def slot(h, par, dot=None, look=None, mlp=None):
                dense_to_feat(h, par)
                for v in range(GUNITS):
                    if dot:
                        dots_to_sbuf(*dot, v)
                    if v in ROWS_IN_DOTS:
                        transposed_to_feat(h, par, ROWS_IN_DOTS[v])
                for u in range(NO):
                    if look:
                        looked_up_to_feat(*look, u)
                    if mlp:
                        mlp_step(*mlp, u)
                    if u in ROWS_IN_LOOKUPS:
                        transposed_to_feat(h, par, ROWS_IN_LOOKUPS[u])

            split_hi(0)
            split_hi(1)
            for u in range(NO):
                if u + 2 < NO:
                    split_hi(u + 2)
                looked_up_to_feat(0, 0, u)
            slot(0, 0, look=(0, 1))
            slot(0, 1, dot=(0, 0), look=(1, 0))
            act.wait_ge(weights_loaded, WEIGHT_DMAS * DMA)
            act.wait_ge(w1_summed, 1)
            with act.Fori(1, NCH // 2 - 1) as h:
                slot(h, 0, dot=(h - 1, 1), look=(h, 1), mlp=(h - 1, 0))
                slot(h, 1, dot=(h, 0), look=(h + 1, 0), mlp=(h - 1, 1))
            last = NCH // 2 - 1
            slot(last, 0, dot=(last - 1, 1), look=(last, 1), mlp=(last - 1, 0))
            dense_to_feat(last, 1)
            for v in range(GUNITS):
                dots_to_sbuf(last, 0, v)
                if v in ROWS_IN_DOTS:
                    transposed_to_feat(last, 1, ROWS_IN_DOTS[v])
            for u in range(NO):
                mlp_step(last - 1, 1, u)
                if u in ROWS_IN_LOOKUPS:
                    transposed_to_feat(last, 1, ROWS_IN_LOOKUPS[u])
            for v in range(GUNITS):
                dots_to_sbuf(last, 1, v)
            for u in range(NO):
                mlp_step(last, 0, u)
            for u in range(NO):
                mlp_step(last, 1, u)

        @block.vector
        def _(dve):
            nc.vector.memset(feat[:, 1, :, :, NF:FS], 0.0).then_inc(pads_zeroed, 1)
            dve.wait_ge(iotas_made, 1)
            nc.vector.tensor_copy(row_f[:], row_i[:]).then_inc(row_f_made, 1)
            nc.vector.tensor_scalar(ident[:], diag, 0.0, None, ALU.is_equal).then_inc(ident_made, 1)
            dve.wait_ge(row_f_made, 1)

            def split_lo(u):
                dve.wait_ge(hi_made, u + 1)
                nc.vector.tensor_tensor(table_lo[0:TP, u, :], raw_table(u)[0:TP],
                                        table_hi[0:TP, u, :].bitcast(fp32), ALU.subtract).then_inc(lo_made, 1)

            def shift_ids(h, par, j):
                a, b = IDS[j]
                dve.wait_ge(ids_loaded[j], DMA * (chunk(h, par) + 1))
                nc.vector.tensor_scalar(ids_local[:, a:b, :], ids_bc[:, a:b, :], row_f[:, 0:1], None,
                                        ALU.subtract).then_inc(ids_shifted, 1)
                dve.wait_ge(ids_shifted, chunk(h, par) * len(IDS) + j + 1)

            def make_onehot(h, par, u, c0=0, c1=RPP):
                n = chunk(h, par)
                if c0 == 0 and u in [a for a, b in IDS]:
                    shift_ids(h, par, [a for a, b in IDS].index(u))
                if c0 == 0 and not (isinstance(n, int) and n == 0 and u < 2):
                    dve.wait_ge(looked_up, n * NO + u - 1)
                for c in range(c0, c1):
                    last = nc.vector.tensor_scalar(onehot[0:TP, (NO * par + u) % 2, c, :],
                                                   ids_local[0:TP, u, :], float(c), None, ALU.is_equal)
                if c1 == RPP:
                    last.then_inc(onehot_made, 1)

            def dots_to_sbuf(h, par, v):
                dve.wait_ge(dots_done, chunk(h, par) * GUNITS + v + 1)
                for q in range(Q // 2, Q):
                    last = nc.vector.tensor_copy(*dot_copy(par, v, q))
                last.then_inc(dots_out_dve, 1)

            def slot(dot=None, look=None):
                for v in range(GUNITS):
                    if dot:
                        dots_to_sbuf(*dot, v)
                    if look and v >= GUNITS - 4:
                        u, half = divmod(v - (GUNITS - 4), 2)
                        make_onehot(*look, u, half * RPP // 2, (half + 1) * RPP // 2)
                if look:
                    for u in range(2, NO):
                        make_onehot(*look, u)

            for u in range(NO):
                split_lo(u)
                make_onehot(0, 0, u)
                if u == 1:
                    nc.vector.memset(feat[:, 0, :, :, NF:FS], 0.0).then_inc(pads0_zeroed, 1)
            slot(look=(0, 1))
            dve.wait_ge(weights_loaded, WEIGHT_DMAS * DMA)
            nc.vector.tensor_tensor(w1_sb[:, ZC, :], w1_sb[:, ZC, :], w1_dense2, ALU.add).then_inc(w1_summed, 1)
            slot(dot=(0, 0), look=(1, 0))
            with dve.Fori(1, NCH // 2 - 1) as h:
                slot(dot=(h - 1, 1), look=(h, 1))
                slot(dot=(h, 0), look=(h + 1, 0))
            last = NCH // 2 - 1
            slot(dot=(last - 1, 1), look=(last, 1))
            slot(dot=(last, 0))
            slot(dot=(last, 1))

        @block.tensor
        def _(pe):
            def is_first(h, par, u=0):
                return isinstance(h, int) and h == 0 and par == 0 and u == 0

            def transposes(h, par, u):
                pe.wait_ge(rows_loaded[u], DMA * len(UNIT[u]) * TILES * (chunk(h, par) + 1))
                if not is_first(h, par, u):
                    pe.wait_ge(transposed_out, chunk(h, par) * UNITS + u)
                for k in range(len(UNIT[u])):
                    for t in range(TILES):
                        last = nc.tensor.transpose(tr_ps[:, k, t * P:(t + 1) * P], rows[:, u, k, t, :], ident[:])
                last.then_inc(transposed, 1)

            def lookup(h, par, u):
                n = chunk(h, par)
                if isinstance(n, int) and n == 0:
                    pe.wait_ge(lo_made, u + 1)
                pe.wait_ge(onehot_made, n * NO + u + 1)
                if not is_first(h, par, u):
                    pe.wait_ge(looked_up_out, n * NO + u)
                for part in (table_lo, table_hi):
                    for c in range(RPP):
                        last = nc.tensor.matmul(oh_ps[:, 0:CH], part[0:TP, u, c * D:(c + 1) * D],
                                                onehot[0:TP, (NO * par + u) % 2, c, :],
                                                start=(part is table_lo and c == 0),
                                                stop=(part is table_hi and c == RPP - 1))
                last.then_inc(looked_up, 1)

            def dot_products(h, par, v):
                n = chunk(h, par)
                if v == 0:
                    pe.wait_ge(transposed_out, UNITS * (n + 1))
                    pe.wait_ge(looked_up_out, NO * (n + 1))
                    pe.wait_ge(dense_out, n + 1)
                if not (isinstance(n, int) and n == 0 and v < 2):
                    pe.wait_ge(dots_out_act, n * GUNITS + v - 1)
                    pe.wait_ge(dots_out_dve, n * GUNITS + v - 1)
                for k in range(2):
                    for gi in range(GPU // 2):
                        g = v * GPU + k * (GPU // 2) + gi
                        last = nc.tensor.matmul(dot_ps[0:FS * (Q - 1) + NI, v % 2, k, gi * Q * NJ:(gi + 1) * Q * NJ],
                                                feat[:, par, g].rearrange("p q f -> p (q f)")[:, 0:FS * (Q - 1) + NI],
                                                feat[:, par, g, :, 1:NF],
                                                start=True, stop=True)
                last.then_inc(dots_done, 1)

            def layer1(h, par, x, last_chunk=False):
                n = chunk(h, par)
                first = isinstance(n, int) and n == 0
                if x == 0:
                    pe.wait_ge(z_loaded, DMA * (Z_DMAS * n + (1 if last_chunk else Z_DMAS)))
                    if last_chunk:
                        pe.wait_ge(pairs_gathered, DMA * ZC)
                    if not first:
                        pe.wait_ge(y_made, n)
                if x == 1 and not first:
                    pe.wait_ge(h2_made, n * (N2 // P))
                if x >= 2:
                    pe.wait_ge(h1_made, n * (N1 // P) + x - 1)
                for c in range(ZC + 1):
                    m = PAIRS - c * P if c == ZC - 1 else P
                    last = nc.tensor.matmul(mlp_ps[:, x % 2, 0:CH], w1_sb[0:m, c, x * P:(x + 1) * P],
                                            zt[0:m, c, :], start=(c == 0), stop=(c == ZC))
                last.then_inc(l1_done, 1)

            def layer2(h, par):
                pe.wait_ge(h1_made, (N1 // P) * (chunk(h, par) + 1))
                for x in range(N2 // P):
                    for c in range(N1 // P):
                        last = nc.tensor.matmul(mlp_ps[:, x, 0:CH], w2_sb[:, c, x * P:(x + 1) * P],
                                                h1[:, c, :], start=(c == 0), stop=(c == N1 // P - 1))
                    last.then_inc(l2_done, 1)

            def layer3(h, par):
                pe.wait_ge(h2_made, (N2 // P) * (chunk(h, par) + 1))
                for t in range(TILES):
                    for c in range(N2 // P):
                        last = nc.tensor.matmul(mlp_ps[:, 0, t:t + 1], h2[:, c, t * P:(t + 1) * P],
                                                w3_sb[:, c:c + 1], start=(c == 0), stop=(c == N2 // P - 1))
                last.then_inc(l3_done, 1)

            def mlp_step(h, par, u, last_chunk=False):
                if u < N1 // P:
                    layer1(h, par, u, last_chunk)
                if u == LAYER2_AT:
                    layer2(h, par)
                if u == LAYER3_AT:
                    layer3(h, par)

            def slot(h, par, dot=None, look=None, mlp=None):
                for v in range(GUNITS):
                    if dot:
                        dot_products(*dot, v)
                    if v in ROWS_IN_DOTS:
                        transposes(h, par, ROWS_IN_DOTS[v])
                for u in range(NO):
                    if look:
                        lookup(*look, u)
                    if mlp:
                        mlp_step(*mlp, u)
                    if u in ROWS_IN_LOOKUPS:
                        transposes(h, par, ROWS_IN_LOOKUPS[u])

            for u in range(NO):
                lookup(0, 0, u)
            pe.wait_ge(ident_made, 1)
            slot(0, 0, look=(0, 1))
            pe.wait_ge(pads0_zeroed, 1)
            slot(0, 1, dot=(0, 0), look=(1, 0))
            pe.wait_ge(weights_loaded, WEIGHT_DMAS * DMA)
            pe.wait_ge(w1_summed, 1)
            with pe.Fori(1, NCH // 2 - 1) as h:
                slot(h, 0, dot=(h - 1, 1), look=(h, 1), mlp=(h - 1, 0))
                slot(h, 1, dot=(h, 0), look=(h + 1, 0), mlp=(h - 1, 1))
            last = NCH // 2 - 1
            slot(last, 0, dot=(last - 1, 1), look=(last, 1), mlp=(last - 1, 0))
            for v in range(GUNITS):
                dot_products(last, 0, v)
                if v in ROWS_IN_DOTS:
                    transposes(last, 1, ROWS_IN_DOTS[v])
            for u in range(NO):
                mlp_step(last - 1, 1, u)
                if u in ROWS_IN_LOOKUPS:
                    transposes(last, 1, ROWS_IN_LOOKUPS[u])
            for v in range(GUNITS):
                dot_products(last, 1, v)
            for u in range(NO):
                mlp_step(last, 0, u)
            for u in range(NO):
                mlp_step(last, 1, u, last_chunk=True)


def kernel(**inputs):
    import numpy as np
    import concourse.bacc as bacc
    from concourse.bass_utils import run_bass_kernel_spmd

    nc = bacc.Bacc("TRN2", target_bir_lowering=False, num_devices=1)
    ids = np.ascontiguousarray(inputs["ids"])
    dense = np.asarray(inputs["r_dense_features"])
    pair_idx = np.zeros((P, ZC), np.int32)
    for i, j, m, block, p0 in RUNS:
        pair_idx[p0:p0 + m, block] = i * NJ + j + np.arange(m)
    arrays = {
        "dense_t": dense.reshape(NCH, CH, D).transpose(0, 2, 1),
        "idx": ids[:, GATHERED].reshape(NCH, TILES, P, NG).transpose(0, 2, 3, 1).reshape(NCH, P, NG * TILES),
        "pair_idx": pair_idx,
        "ids_t": ids[:, ONEHOT].reshape(NCH, CH, NO).transpose(0, 2, 1),
    }
    for f in range(F):
        arrays[f"tbl_{f}"] = inputs[f"tbl_{f}"]
    arrays["W_top1"], arrays["W_top2"] = inputs["W_top1"], inputs["W_top2"]
    for name in ("b_top1", "b_top2", "W_top3"):
        arrays[name] = np.asarray(inputs[name]).reshape(-1, P).T
    arrays = {name: np.ascontiguousarray(a) for name, a in arrays.items()}
    aps = {name: nc.dram_tensor(name + "_dram", a.shape, mybir.dt.from_np(a.dtype), kind="ExternalInput").ap()
           for name, a in arrays.items()}
    y = nc.dram_tensor("y_dram", (P, B // P), mybir.dt.float32, kind="ExternalOutput").ap()
    dlrm_tower(nc, aps["dense_t"], aps["idx"], aps["pair_idx"], aps["ids_t"], [aps[f"tbl_{f}"] for f in range(F)],
               aps["W_top1"], aps["b_top1"], aps["W_top2"], aps["b_top2"], aps["W_top3"], y)
    r = run_bass_kernel_spmd(nc, [{name + "_dram": a for name, a in arrays.items()}], core_ids=[0])
    return r.results[0]["y_dram"].T.reshape(B, 1)
```

```python
import concourse.bass as bass
from concourse import mybir
from concourse.alu_op_type import AluOpType as ALU
from contextlib import ExitStack

B, F, D = 2048, 26, 128
ROWS = [1000, 1000, 125000, 1250, 1000, 12500, 12500, 12500, 1000, 1000, 1000, 12500, 1000,
        1250, 12500, 12500, 1000, 1250, 12500, 1000, 12500, 1000, 12500, 1250, 1000, 1000]
N1, N2 = 512, 256
P = 128

NF = F + 1
SMALL = min(ROWS)
LOOKUPS = (8, 7)
NO = max(LOOKUPS)
ONEHOT = [f for f in range(F) if ROWS[f] == SMALL][:NO]
GATHERED = [[f for f in range(F) if f not in ONEHOT[:k]] for k in LOOKUPS]

CH = 256
TILES = CH // P
NCH = B // CH
Q = 4
NI = NF
QS = CH // Q
UNITS = -(-max(len(fs) for fs in GATHERED) // 2)
NR = 2 * UNITS - 1


def units(fs):
    pairs = len(fs) - UNITS
    return [fs[2 * u:2 * u + 2] for u in range(pairs)] + [[f] for f in fs[2 * pairs:]]


UNIT = [units(fs) for fs in GATHERED]
RPP = 8
TP = SMALL // RPP
FS = 32
GPU = 8
GUNITS = QS // GPU
NJ = NF - 1
PAIRS = NF * (NF - 1) // 2
DIST = NF // 2
ZC = -(-PAIRS // P)
ZR = PAIRS // ZC
ZI = ZR // DIST
IDS = [[(0, 1), (1, 4), (4, k)] for k in LOOKUPS]
LAYER2, LAYER3 = 4, 5
START = ["i0 s0 s1 i1 l0 s2 l1 s3 i2 l2 s4 l3 s5 r0 l4 s6 l5",
         "s7 r1 i0 i1 l6 r2 l7 r3 f",
         "l0 i2 r4 l1 r5 l2 l3 r6 l4 r7 l5 r8 l6 r9"]
SLOT1 = "d0 i0 d1 i1 d2 i2 d3 d4 r0 d5 d6 d7 r1 l0 r2 l1 l2 r3 f l3 r4 l4 l5 m0 r5 m1 r6 m2 l6 m3 r7 m4 r8 l7 m5 r9"
SLOT = ["d0 i0 d1 i1 d2 i2 r0 d3 d4 d5 r1 d6 d7 r2 l0 l1 r3 l2 f l3 r4 l4 r5 l5 m0 r6 m1 r7 m2 r8 m3 m4 r9 l6 m5",
        "d0 i0 d1 i1 d2 i2 r0 d3 d4 d5 r1 d6 d7 r2 l0 l1 r3 l2 f l3 r4 l4 r5 l5 l6 m0 r6 m1 r7 m2 r8 m3 m4 r9 l7 m5"]
SLOT_BEFORE_LAST = SLOT[0].replace(" m4", "").replace(" m5", "")
SLOT_LAST = "r0 d0 r1 d1 r2 d2 r3 d3 r4 d4 r5 d5 r6 d6 f r7 d7"
DOTS = "d0 d1 d2 d3 d4 d5 d6 d7"
MLP = "m0 m1 m2 m3 m4 m5"
WEIGHT_DMAS = ZC + 6
DMA = 16


def steps(order):
    return [(step[0], int(step[1:] or 0)) for step in order.split()]


def before(h, par):
    return sum(LOOKUPS) * h + sum(LOOKUPS[:par])


def following(h, par):
    return (h, 1) if par == 0 else (h + 1, 0)


def pair(row):
    i, d = divmod(row, DIST)
    if i == NF - 1:
        return NJ - DIST + d, NF - 1
    i, j = divmod(i * (NJ + 1) + d + 1, NJ)
    return min(i, j), max(i, j)


assert sorted(pair(row) for row in range(PAIRS)) == [(a, b) for a in range(NF) for b in range(a + 1, NF)]
Z_DMAS = ZC + 2


def dlrm_tower(nc, dense_t, idx, ids_t, tables, w1, b1, w2, b2, w3, y):
    fp32, fp32r, i32 = mybir.dt.float32, mybir.dt.float32r, mybir.dt.int32
    ACT = mybir.ActivationFunctionType
    dots_dram = nc.dram_tensor("dots_scratch", (2, NI * (NJ + 1), CH), fp32, kind="Internal").ap()

    ctx = ExitStack()
    with ctx:
        def sb(name, shape, dt):
            return ctx.enter_context(nc.sbuf_tensor(name, shape, dt))

        def ps(name, shape, dt):
            return ctx.enter_context(nc.psum_tensor(name, shape, dt))

        def sem(name):
            return ctx.enter_context(nc.semaphore(name))

        feat = sb("feat", [P, 2, QS, Q, FS], fp32)
        table_hi = sb("table_hi", [P, NO, RPP * D], fp32r)
        table_lo = sb("table_lo", [P, NO, RPP * D], fp32r)
        onehot = sb("onehot", [P, 2, RPP, CH], fp32r)
        ids_bc = sb("ids_bc", [P, NO, CH], i32)
        rows = sb("rows", [P, NR, TILES, D], fp32)
        dense_sb = sb("dense_sb", [P, CH], fp32)
        idx_sb = sb("idx_sb", [P, 2, NR * TILES], i32)
        dots = sb("dots", [P, NJ * QS], fp32)
        zt = sb("zt", [P, ZC + 1, CH], fp32)
        w1_sb = sb("w1_sb", [P, ZC + 1, N1], fp32)
        w2_sb = sb("w2_sb", [P, N1 // P, N2], fp32)
        w3_sb = sb("w3_sb", [P, N2 // P], fp32)
        b1_sb = sb("b1_sb", [P, N1 // P], fp32)
        b2_sb = sb("b2_sb", [P, N2 // P], fp32)
        h1 = sb("h1", [P, N1 // P, CH], fp32)
        h2 = sb("h2", [P, N2 // P, CH], fp32)
        y_sb = sb("y_sb", [P, B // P], fp32)
        row_i = sb("row_i", [P, 1], i32)
        row_f = sb("row_f", [P, 1], fp32)
        ident = sb("ident", [P, P], fp32)
        ids_local = ids_bc[:].bitcast(fp32)
        diag = h1[:, 2, 0:P].bitcast(i32)
        w1_dense2 = h1[:, 0:2, :].rearrange("p a b -> p (a b)")

        feat1 = feat[:, 1].rearrange("p g q f -> p (g q f)")

        def raw_table(u):
            if u == 0:
                return dots[:, 0:RPP * D]
            if u == NO - 1:
                return zt[:].rearrange("p c b -> p (c b)")
            return feat1[:, (u - 1) * RPP * D:u * RPP * D]

        tr_ps = ps("tr_ps", [P, 2, CH], fp32)
        oh_ps = ps("oh_ps", [P, 512], fp32)
        dot_ps = ps("dot_ps", [P, 2, 2, 512], fp32)
        mlp_ps = ps("mlp_ps", [P, 2, 512], fp32)

        def lookup_place(u):
            return u % 2

        def lookup_back(par, u):
            return 1 if par == 0 and u == 0 else 2

        def lookup_psum(u):
            return dot_ps[:, 0, 1, 0:CH] if lookup_place(u) else oh_ps[:, 0:CH]

        idx_loaded = [sem(f"idx_loaded{p}") for p in range(2)]
        ids_loaded = [sem(f"ids_loaded{j}") for j in range(len(IDS[0]))]
        rows_loaded = [sem(f"rows_loaded{u}") for u in range(UNITS)]
        dense_loaded = sem("dense_loaded")
        table_loaded = [sem(f"table_loaded{u}") for u in range(NO)]
        dense_out = sem("dense_out")
        weights_loaded = sem("weights_loaded")
        slot_free = sem("slot_free")
        pads_zeroed = sem("pads_zeroed")
        pads0_zeroed = sem("pads0_zeroed")
        iotas_made = sem("iotas_made")
        ids_shifted = sem("ids_shifted")
        row_f_made = sem("row_f_made")
        ident_made = sem("ident_made")
        hi_made = sem("hi_made")
        lo_made = sem("lo_made")
        w1_summed = sem("w1_summed")
        onehot_made = sem("onehot_made")
        transposed = sem("transposed")
        transposed_out = sem("transposed_out")
        looked_up = sem("looked_up")
        looked_up_out = sem("looked_up_out")
        dots_done = sem("dots_done")
        dots_out_act = sem("dots_out_act")
        dots_out_dve = sem("dots_out_dve")
        dots_stored = sem("dots_stored")
        z_loaded = sem("z_loaded")
        l1_done = sem("l1_done")
        h1_made = sem("h1_made")
        l2_done = sem("l2_done")
        h2_made = sem("h2_made")
        l3_done = sem("l3_done")
        y_made = sem("y_made")
        y_stored = sem("y_stored")

        def chunk(h, par):
            return 2 * h + par

        def feat_view(par, f0, nf, step):
            v = feat[:, par].rearrange("p g q f -> p f q g")
            return v[:, f0:f0 + step * (nf - 1) + 1:step]

        def dots_of(h, par):
            if isinstance(h, int) and chunk(h, par) == NCH - 1:
                return rows[:].rearrange("p f t d -> p (f t d)")[:, 0:NJ * QS]
            return dots[:]

        def dot_copy(h, par, v, q):
            p = slice(32 * q, 32 * q + NI)
            dst = dots_of(h, par)[p].rearrange("p (j g) -> p g j", j=NJ)[:, v * GPU:(v + 1) * GPU, :]
            src = dot_ps[p, v % 2, :, 0:GPU // 2 * Q * NJ].rearrange("p k (g q j) -> p k g q j", q=Q, j=NJ)
            return dst.rearrange("p (k g) j -> p k g j", k=2), src[:, :, :, q, :]

        block = ctx.enter_context(nc.Block())

        @block.sync
        def _(sp):
            def load_idx(h, par):
                sp.dma_start(idx_sb[:, par, :], idx[bass.ds(chunk(h, par), 1)].rearrange("a p x -> (a p) x")
                             ).then_inc(idx_loaded[par], DMA)

            def load_ids(h, par, j):
                a, b = IDS[par][j]
                src = ids_t[bass.ds(chunk(h, par), 1), a:b, :].rearrange("a f b -> a (f b)")
                sp.dma_start(ids_bc[:, a:b, :].rearrange("p f b -> p (f b)"),
                             src.broadcast_to([P, (b - a) * CH])).then_inc(ids_loaded[j], DMA)

            def load_dense(h, par):
                sp.dma_start(dense_sb[:], dense_t[bass.ds(chunk(h, par), 1)].rearrange("a p b -> (a p) b")
                             ).then_inc(dense_loaded, DMA)

            def load_table(u):
                raw = raw_table(u)
                src = tables[ONEHOT[u]].rearrange("(r c) d -> r (c d)", c=RPP)
                sp.dma_start(raw[0:120], src[0:120]).then_inc(table_loaded[u], DMA)
                sp.dma_start(raw[120:TP], src[120:TP]).then_inc(table_loaded[u], DMA)

            def next_dense(h, par):
                sp.wait_ge(dense_out, chunk(h, par) + 1)
                load_dense(*following(h, par))

            def next_ids(h, par):
                for j in range(len(IDS[0])):
                    sp.wait_ge(onehot_made, before(*following(h, par)) + IDS[1 - par][j][1])
                    load_ids(h + 1, par, j)

            def next_idx(h, par):
                sp.wait_ge(transposed, (chunk(h, par) + 1) * UNITS)
                load_idx(h + 1, par)

            def make_z(h, par):
                n = chunk(h, par)
                sp.wait_ge(dots_out_act, GUNITS * (n + 1))
                sp.wait_ge(dots_out_dve, GUNITS * (n + 1))
                products = dots_dram[par, 0:NI * NJ, :].rearrange("(i j) b -> i j b", j=NJ)
                for q in range(Q):
                    sp.dma_start(products[:, :, q * QS:(q + 1) * QS],
                                 dots_of(h, par)[32 * q:32 * q + NI].rearrange("p (j g) -> p j g", j=NJ)
                                 ).then_inc(dots_stored, DMA)
                if not (isinstance(n, int) and n == 0):
                    sp.wait_ge(l1_done, N1 // P * n)
                sp.dma_start(zt[:, ZC, :], dense_t[bass.ds(n, 1)].rearrange("a p b -> (a p) b")
                             ).then_inc(z_loaded, DMA)
                sp.wait_ge(dots_stored, Q * DMA * (n + 1))
                for c in range(ZC):
                    i0, m = c * ZI, min(ZI, NF - 1 - c * ZI)
                    runs = dots_dram[par, i0 * (NJ + 1) + 1:(i0 + m) * (NJ + 1) + 1, :]
                    sp.dma_start(zt[0:m * DIST, c, :],
                                 runs.rearrange("(i d) b -> i d b", d=NJ + 1)[:, 0:DIST, :]
                                 ).then_inc(z_loaded, DMA)
                sp.dma_start(zt[ZR - DIST:ZR, ZC - 1, :], dots_dram[par, NI * NJ - DIST:NI * NJ, :]
                             ).then_inc(z_loaded, DMA)

            load_idx(0, 0)
            load_ids(0, 0, 0)
            load_table(0)
            sp.wait_ge(pads_zeroed, 1)
            load_table(1)
            load_ids(0, 0, 1)
            for u in range(2, 5):
                load_table(u)
            load_ids(0, 0, 2)
            for u in range(5, NO):
                load_table(u)
            load_dense(0, 0)
            load_idx(0, 1)
            for j in range(len(IDS[0])):
                sp.wait_ge(onehot_made, IDS[0][j][1])
                load_ids(0, 1, j)
            next_dense(0, 0)
            next_ids(0, 0)
            next_idx(0, 0)
            for c in range(ZC):
                sp.dma_start(w1_sb[0:ZR, c, :], w1[D + c * ZR:D + (c + 1) * ZR, :]).then_inc(weights_loaded, DMA)
            sp.dma_start(w1_sb[:, ZC, :], w1[0:D, :]).then_inc(weights_loaded, DMA)
            sp.wait_ge(ident_made, 1)
            sp.dma_start(w1_dense2, w1[D + PAIRS:, :]).then_inc(weights_loaded, DMA)
            sp.dma_start(w2_sb[:], w2.rearrange("(c p) n -> p c n", p=P)).then_inc(weights_loaded, DMA)
            sp.dma_start(w3_sb[:], w3).then_inc(weights_loaded, DMA)
            sp.dma_start(b1_sb[:], b1).then_inc(weights_loaded, DMA)
            sp.dma_start(b2_sb[:], b2).then_inc(weights_loaded, DMA)
            make_z(0, 0)
            next_dense(0, 1)
            next_ids(0, 1)
            next_idx(0, 1)
            with sp.Fori(1, NCH // 2 - 1) as h:
                make_z(h - 1, 1)
                next_dense(h, 0)
                next_ids(h, 0)
                next_idx(h, 0)
                make_z(h, 0)
                next_dense(h, 1)
                next_ids(h, 1)
                next_idx(h, 1)
            last = NCH // 2 - 1
            make_z(last - 1, 1)
            next_dense(last, 0)
            make_z(last, 0)
            make_z(last, 1)
            sp.wait_ge(y_made, NCH)
            sp.dma_start(y, y_sb[:]).then_inc(y_stored, DMA)
            sp.wait_ge(y_stored, DMA)

        @block.gpsimd
        def _(pool):
            nc.gpsimd.iota(row_i[:], [[1, 1]], base=0, channel_multiplier=-RPP)
            nc.gpsimd.iota(diag, [[1, P]], base=0, channel_multiplier=-1).then_inc(iotas_made, 1)

            def gathers(h, par):
                pool.wait_ge(idx_loaded[par], DMA * (h + 1))
                pool.sem_inc(slot_free, 1)
                for u in range(UNITS):
                    if not (isinstance(h, int) and h == 0 and par == 0):
                        pool.wait_ge(transposed, (chunk(h, par) - 1) * UNITS + u + 1)
                        pool.sem_inc(slot_free, 1)
                    for k in range(len(UNIT[par][u])):
                        g = 2 * u + k
                        for t in range(TILES):
                            nc.gpsimd.indirect_dma_start(
                                rows[:, g, t, :], None, tables[UNIT[par][u][k]],
                                bass.IndirectOffsetOnAxis(
                                    ap=idx_sb[:, par, g * TILES + t:g * TILES + t + 1], axis=0),
                            ).then_inc(rows_loaded[u], DMA)

            gathers(0, 0)
            gathers(0, 1)
            with pool.Fori(1, NCH // 2) as h:
                gathers(h, 0)
                gathers(h, 1)

        @block.scalar
        def _(act):
            def split_hi(u):
                act.wait_ge(table_loaded[u], 2 * DMA)
                nc.scalar.activation(table_hi[0:TP, u, :], raw_table(u)[0:TP], ACT.Copy).then_inc(hi_made, 1)

            def shift_ids(h, par, j):
                a, b = IDS[par][j]
                if isinstance(h, int) and h == 0 and par == 0 and j == 0:
                    act.wait_ge(row_f_made, 1)
                act.wait_ge(ids_loaded[j], DMA * (chunk(h, par) + 1))
                nc.scalar.activation(ids_local[:, a:b, :], ids_bc[:, a:b, :], ACT.Identity,
                                     bias=row_f[:, 0:1]).then_inc(ids_shifted, 1)

            def dense_to_feat(h, par):
                act.wait_ge(dense_loaded, DMA * (chunk(h, par) + 1))
                nc.scalar.activation(feat_view(par, 0, 1, 1)[:, 0],
                                     dense_sb[:].rearrange("p (q g) -> p q g", q=Q),
                                     ACT.Copy).then_inc(dense_out, 1)

            def transposed_to_feat(h, par, u):
                act.wait_ge(transposed, chunk(h, par) * UNITS + u + 1)
                fs = UNIT[par][u]
                m, step = len(fs), fs[-1] - fs[0]
                nc.scalar.activation(feat_view(par, fs[0] + 1, m, max(step, 1)),
                                     tr_ps[:, 0:m].rearrange("p f (q g) -> p f q g", q=Q),
                                     ACT.Copy).then_inc(transposed_out, 1)

            def looked_up_to_feat(h, par, u):
                act.wait_ge(looked_up, before(h, par) + u + 1)
                nc.scalar.activation(feat_view(par, ONEHOT[u] + 1, 1, 1)[:, 0],
                                     lookup_psum(u).rearrange("p (q g) -> p q g", q=Q),
                                     ACT.Copy).then_inc(looked_up_out, 1)

            def dots_to_sbuf(h, par, v):
                n = chunk(h, par)
                act.wait_ge(dots_done, n * GUNITS + v + 1)
                if v == 0 and not (isinstance(n, int) and n in (0, NCH - 1)):
                    act.wait_ge(dots_stored, Q * DMA * n)
                for q in range(Q // 2):
                    last = nc.scalar.activation(*dot_copy(h, par, v, q), ACT.Copy)
                last.then_inc(dots_out_act, 1)

            def relu1(h, par, x):
                if isinstance(h, int) and h == 0 and par == 0 and x == 0:
                    act.wait_ge(weights_loaded, WEIGHT_DMAS * DMA)
                    act.wait_ge(w1_summed, 1)
                act.wait_ge(l1_done, chunk(h, par) * (N1 // P) + x + 1)
                nc.scalar.activation(h1[:, x, :], mlp_ps[:, x % 2, 0:CH], ACT.Relu,
                                     bias=b1_sb[:, x:x + 1]).then_inc(h1_made, 1)

            def relu2(h, par, x):
                act.wait_ge(l2_done, chunk(h, par) * (N2 // P) + x + 1)
                nc.scalar.activation(h2[:, x, :], mlp_ps[:, x, 0:CH], ACT.Relu,
                                     bias=b2_sb[:, x:x + 1]).then_inc(h2_made, 1)

            def output(h, par):
                n = chunk(h, par)
                act.wait_ge(l3_done, n + 1)
                nc.scalar.activation(y_sb[:, bass.ds(n * TILES, TILES)], mlp_ps[:, 0, 0:TILES],
                                     ACT.Copy).then_inc(y_made, 1)

            def mlp_step(h, par, step):
                if step < LAYER2:
                    relu1(h, par, step)
                if step == LAYER2:
                    for x in range(N2 // P):
                        relu2(h, par, x)
                if step == LAYER3:
                    output(h, par)

            def run(order, rows=None, done=None, look=None, ids=None):
                for kind, x in steps(order):
                    if kind == "i":
                        shift_ids(*(ids or look), x)
                    if kind == "d":
                        dots_to_sbuf(*done, x)
                    if kind == "r":
                        transposed_to_feat(*rows, x)
                    if kind == "f":
                        dense_to_feat(*rows)
                    if kind == "l":
                        looked_up_to_feat(*look, x)
                    if kind == "s":
                        split_hi(x)
                    if kind == "m":
                        mlp_step(*done, x)

            act.wait_ge(iotas_made, 1)
            nc.scalar.activation(row_f[:], row_i[:], ACT.Copy).then_inc(row_f_made, 1)
            run(START[0], rows=(0, 0), look=(0, 0))
            run(START[1], rows=(0, 0), look=(0, 0), ids=(0, 1))
            run(START[2], rows=(0, 0), look=(0, 1))
            run(SLOT1, rows=(0, 1), done=(0, 0), look=(1, 0))
            with act.Fori(1, NCH // 2 - 1) as h:
                run(SLOT[0], rows=(h, 0), done=(h - 1, 1), look=(h, 1))
                run(SLOT[1], rows=(h, 1), done=(h, 0), look=(h + 1, 0))
            last = NCH // 2 - 1
            run(SLOT_BEFORE_LAST, rows=(last, 0), done=(last - 1, 1), look=(last, 1))
            run(SLOT_LAST, rows=(last, 1), done=(last, 0))
            run("m4 r8 m5 r9", rows=(last, 1), done=(last - 1, 1))
            run(DOTS, done=(last, 1))
            run(MLP, done=(last, 0))
            run(MLP, done=(last, 1))

        @block.vector
        def _(dve):
            nc.vector.memset(feat[:, 1, :, :, NF:FS], 0.0).then_inc(pads_zeroed, 1)
            dve.wait_ge(iotas_made, 1)
            nc.vector.tensor_scalar(ident[:], diag, 0.0, None, ALU.is_equal).then_inc(ident_made, 1)
            nc.vector.memset(feat[:, 0, :, :, NF:FS], 0.0).then_inc(pads0_zeroed, 1)

            def split_lo(u):
                dve.wait_ge(hi_made, u + 1)
                nc.vector.tensor_tensor(table_lo[0:TP, u, :], raw_table(u)[0:TP],
                                        table_hi[0:TP, u, :].bitcast(fp32), ALU.subtract).then_inc(lo_made, 1)

            def make_onehot(h, par, u, c0=0, c1=RPP):
                starts = [a for a, b in IDS[par]]
                if c0 == 0 and u in starts:
                    dve.wait_ge(ids_shifted, chunk(h, par) * len(IDS[0]) + starts.index(u) + 1)
                if c0 == 0 and not (isinstance(h, int) and h == 0 and par == 0 and u < 2):
                    dve.wait_ge(looked_up, before(h, par) + u + 1 - lookup_back(par, u))
                for c in range(c0, c1):
                    last = nc.vector.tensor_scalar(onehot[0:TP, lookup_place(u), c, :],
                                                   ids_local[0:TP, u, :], float(c), None, ALU.is_equal)
                if c1 == RPP:
                    last.then_inc(onehot_made, 1)

            def dots_to_sbuf(h, par, v):
                n = chunk(h, par)
                dve.wait_ge(dots_done, n * GUNITS + v + 1)
                if v == 0 and not (isinstance(n, int) and n in (0, NCH - 1)):
                    dve.wait_ge(dots_stored, Q * DMA * n)
                for q in range(Q // 2, Q):
                    last = nc.vector.tensor_copy(*dot_copy(h, par, v, q))
                last.then_inc(dots_out_dve, 1)

            def slot(dot=None, look=None):
                for v in range(GUNITS):
                    if dot:
                        dots_to_sbuf(*dot, v)
                    if look and v >= GUNITS - 4:
                        u, half = divmod(v - (GUNITS - 4), 2)
                        make_onehot(*look, u, half * RPP // 2, (half + 1) * RPP // 2)
                if look:
                    if isinstance(look[0], int) and look == (1, 0):
                        dve.wait_ge(weights_loaded, WEIGHT_DMAS * DMA)
                        nc.vector.tensor_tensor(w1_sb[:, ZC, :], w1_sb[:, ZC, :], w1_dense2,
                                                ALU.add).then_inc(w1_summed, 1)
                    for u in range(2, LOOKUPS[look[1]]):
                        make_onehot(*look, u)

            for u in range(LOOKUPS[0]):
                make_onehot(0, 0, u)
                split_lo(u)
            for u in range(LOOKUPS[1]):
                make_onehot(0, 1, u)
            slot(dot=(0, 0), look=(1, 0))
            with dve.Fori(1, NCH // 2 - 1) as h:
                slot(dot=(h - 1, 1), look=(h, 1))
                slot(dot=(h, 0), look=(h + 1, 0))
            last = NCH // 2 - 1
            slot(dot=(last - 1, 1), look=(last, 1))
            slot(dot=(last, 0))
            slot(dot=(last, 1))

        @block.tensor
        def _(pe):
            def is_first(h, par, u=0):
                return isinstance(h, int) and h == 0 and par == 0 and u == 0

            def transposes(h, par, u):
                loads = [DMA * TILES * len(UNIT[p][u]) for p in range(2)]
                pe.wait_ge(rows_loaded[u], sum(loads) * h + sum(loads[:par + 1]))
                if is_first(h, par, u):
                    pe.wait_ge(ident_made, 1)
                else:
                    pe.wait_ge(transposed_out, chunk(h, par) * UNITS + u)
                for k in range(len(UNIT[par][u])):
                    for t in range(TILES):
                        last = nc.tensor.transpose(tr_ps[:, k, t * P:(t + 1) * P], rows[:, 2 * u + k, t, :], ident[:])
                last.then_inc(transposed, 1)

            def lookup(h, par, u):
                m = before(h, par) + u
                new_table = isinstance(h, int) and h == 0 and par == 0
                if new_table:
                    pe.wait_ge(hi_made, u + 1)
                pe.wait_ge(onehot_made, m + 1)
                if not (isinstance(m, int) and m < 2):
                    pe.wait_ge(looked_up_out, m + 1 - lookup_back(par, u))
                if lookup_place(u) and u < 2 and not (isinstance(h, int) and h == 0):
                    pe.wait_ge(dots_out_act, (chunk(h, par) - 1) * GUNITS - 1)
                    pe.wait_ge(dots_out_dve, (chunk(h, par) - 1) * GUNITS - 1)
                for part in (table_hi, table_lo):
                    if part is table_lo and new_table:
                        pe.wait_ge(lo_made, u + 1)
                    for c in range(RPP):
                        last = nc.tensor.matmul(lookup_psum(u), part[0:TP, u, c * D:(c + 1) * D],
                                                onehot[0:TP, lookup_place(u), c, :],
                                                start=(part is table_hi and c == 0),
                                                stop=(part is table_lo and c == RPP - 1))
                last.then_inc(looked_up, 1)

            def dot_products(h, par, v):
                n = chunk(h, par)
                if v == 0:
                    pe.wait_ge(transposed_out, UNITS * (n + 1))
                    ahead = LOOKUPS[1 - par] - (1 if lookup_place(LOOKUPS[1 - par] - 1) == 0 else 0)
                    if isinstance(n, int) and n == NCH - 1:
                        ahead = 0
                    pe.wait_ge(looked_up_out, before(h, par) + LOOKUPS[par] + ahead)
                    pe.wait_ge(dense_out, n + 1)
                if not (isinstance(n, int) and n == 0 and v < 2):
                    pe.wait_ge(dots_out_act, n * GUNITS + v - 1)
                    pe.wait_ge(dots_out_dve, n * GUNITS + v - 1)
                for k in range(2):
                    for gi in range(GPU // 2):
                        g = v * GPU + k * (GPU // 2) + gi
                        last = nc.tensor.matmul(dot_ps[0:FS * (Q - 1) + NI, v % 2, k, gi * Q * NJ:(gi + 1) * Q * NJ],
                                                feat[:, par, g].rearrange("p q f -> p (q f)")[:, 0:FS * (Q - 1) + NI],
                                                feat[:, par, g, :, 0:NJ],
                                                start=True, stop=True)
                last.then_inc(dots_done, 1)

            def layer1(h, par, x):
                n = chunk(h, par)
                first = isinstance(n, int) and n == 0
                if x == 0:
                    pe.wait_ge(z_loaded, DMA * Z_DMAS * (n + 1))
                    if first:
                        pe.wait_ge(weights_loaded, WEIGHT_DMAS * DMA)
                        pe.wait_ge(w1_summed, 1)
                    else:
                        pe.wait_ge(y_made, n)
                if x == 1 and not first:
                    pe.wait_ge(h2_made, n * (N2 // P))
                if x >= 2:
                    pe.wait_ge(h1_made, n * (N1 // P) + x - 1)
                for c in range(ZC + 1):
                    m = ZR if c < ZC else P
                    last = nc.tensor.matmul(mlp_ps[:, x % 2, 0:CH], w1_sb[0:m, c, x * P:(x + 1) * P],
                                            zt[0:m, c, :], start=(c == 0), stop=(c == ZC))
                last.then_inc(l1_done, 1)

            def layer2(h, par):
                n = chunk(h, par)
                for x in range(N2 // P):
                    for c in range(N1 // P):
                        if x == 0 and c in (0, N1 // P - 1):
                            pe.wait_ge(h1_made, (N1 // P) * (n + 1) - (c == 0))
                        last = nc.tensor.matmul(mlp_ps[:, x, 0:CH], w2_sb[:, c, x * P:(x + 1) * P],
                                                h1[:, c, :], start=(c == 0), stop=(c == N1 // P - 1))
                    last.then_inc(l2_done, 1)

            def layer3(h, par):
                pe.wait_ge(h2_made, (N2 // P) * (chunk(h, par) + 1))
                for t in range(TILES):
                    for c in range(N2 // P):
                        last = nc.tensor.matmul(mlp_ps[:, 0, t:t + 1], h2[:, c, t * P:(t + 1) * P],
                                                w3_sb[:, c:c + 1], start=(c == 0), stop=(c == N2 // P - 1))
                last.then_inc(l3_done, 1)

            def mlp_step(h, par, step):
                if step < LAYER2:
                    layer1(h, par, step)
                if step == LAYER2:
                    layer2(h, par)
                if step == LAYER3:
                    layer3(h, par)

            def run(order, rows=None, done=None, look=None):
                for kind, x in steps(order):
                    if kind == "d":
                        dot_products(*done, x)
                    if kind == "r":
                        transposes(*rows, x)
                    if kind == "l":
                        lookup(*look, x)
                    if kind == "m":
                        mlp_step(*done, x)

            run(START[0], rows=(0, 0), look=(0, 0))
            run(START[1], rows=(0, 0), look=(0, 0))
            run(START[2], rows=(0, 0), look=(0, 1))
            pe.wait_ge(pads0_zeroed, 1)
            run(SLOT1, rows=(0, 1), done=(0, 0), look=(1, 0))
            with pe.Fori(1, NCH // 2 - 1) as h:
                run(SLOT[0], rows=(h, 0), done=(h - 1, 1), look=(h, 1))
                run(SLOT[1], rows=(h, 1), done=(h, 0), look=(h + 1, 0))
            last = NCH // 2 - 1
            run(SLOT_BEFORE_LAST, rows=(last, 0), done=(last - 1, 1), look=(last, 1))
            run(SLOT_LAST, rows=(last, 1), done=(last, 0))
            run("m4 r8 m5 r9", rows=(last, 1), done=(last - 1, 1))
            run(DOTS, done=(last, 1))
            run(MLP, done=(last, 0))
            run(MLP, done=(last, 1))


def kernel(**inputs):
    import numpy as np
    import concourse.bacc as bacc
    from concourse.bass_utils import run_bass_kernel_spmd

    nc = bacc.Bacc("TRN2", target_bir_lowering=False, num_devices=1)
    ids = np.ascontiguousarray(inputs["ids"])
    dense = np.asarray(inputs["r_dense_features"])
    idx = np.zeros((NCH, P, NR, TILES), ids.dtype)
    for n in range(NCH):
        for u, fs in enumerate(UNIT[n % 2]):
            unit_ids = ids[n * CH:(n + 1) * CH, fs].reshape(TILES, P, len(fs))
            idx[n, :, 2 * u:2 * u + len(fs)] = unit_ids.transpose(1, 2, 0)
    place = {ab: row for row, ab in enumerate((a, b) for a in range(NF) for b in range(a + 1, NF))}
    order = np.r_[0:D, [D + place[pair(row)] for row in range(PAIRS)], D + PAIRS:2 * D + PAIRS]
    arrays = {
        "dense_t": dense.reshape(NCH, CH, D).transpose(0, 2, 1),
        "idx": idx.reshape(NCH, P, NR * TILES),
        "ids_t": ids[:, ONEHOT].reshape(NCH, CH, NO).transpose(0, 2, 1),
    }
    for f in range(F):
        arrays[f"tbl_{f}"] = inputs[f"tbl_{f}"]
    arrays["W_top1"], arrays["W_top2"] = np.asarray(inputs["W_top1"])[order], inputs["W_top2"]
    for name in ("b_top1", "b_top2", "W_top3"):
        arrays[name] = np.asarray(inputs[name]).reshape(-1, P).T
    arrays = {name: np.ascontiguousarray(a) for name, a in arrays.items()}
    aps = {name: nc.dram_tensor(name + "_dram", a.shape, mybir.dt.from_np(a.dtype), kind="ExternalInput").ap()
           for name, a in arrays.items()}
    y = nc.dram_tensor("y_dram", (P, B // P), mybir.dt.float32, kind="ExternalOutput").ap()
    dlrm_tower(nc, aps["dense_t"], aps["idx"], aps["ids_t"], [aps[f"tbl_{f}"] for f in range(F)],
               aps["W_top1"], aps["b_top1"], aps["W_top2"], aps["b_top2"], aps["W_top3"], y)
    r = run_bass_kernel_spmd(nc, [{name + "_dram": a for name, a in arrays.items()}], core_ids=[0])
    return r.results[0]["y_dram"].T.reshape(B, 1)
```
